# Optimizing a Trainium2 kernel written in Bass

```python
import numpy as np
import jax
import jax.numpy as jnp

def _softmax(x, axis=-1):
    return jax.nn.softmax(x, axis=axis)
def _gelu(x):
    return jax.nn.gelu(x, approximate=True)
def _silu(x):
    return jax.nn.silu(x)
def _sigmoid(x):
    return jax.nn.sigmoid(x)
def _layernorm(x, axis=-1, eps=1e-5):
    m = jnp.mean(x, axis=axis, keepdims=True)
    v = jnp.var(x, axis=axis, keepdims=True)
    return (x - m) / jnp.sqrt(v + eps)
def _scatter_add(tgt, idx, src, axis=0):
    return tgt.at[idx].add(src)
def _segment_sum(src, seg, n):
    return jax.ops.segment_sum(src, seg, n)

kernel_name = 'mk_conv_seq_d2_conv_nhwc256_4ca787'

def setup_inputs(seed: int = 0):
    np.random.seed(seed)
    _w = jnp.asarray
    def _rec_inputs():
        import jax
        import jax.numpy as jnp
        _gk = jax.random.key(seed)
        x = -0.0003929 + 0.9999 * jax.random.normal(jax.random.fold_in(_gk, 1), (4, 64, 256, 256), jnp.float32)
        return x
    x = _rec_inputs()
    def _L0_conv_setup():
        import jax, jax.numpy as jnp
        import numpy as np
        import math
        B, D_MODEL, EMB, ORDER, SEQ = (4, 64, 33, 64, 256)
        TARGET, FAST_PCT, SLOW_PCT = (0.01, 0.3, 1.5)

        def _pos_emb(L, emb_dim):
            t = jnp.linspace(0.0, 1.0, L)[None, :, None]
            bands = (emb_dim - 1) // 2
            t_r = jnp.linspace(0.0, L - 1.0, L)[None, :, None]
            w = 2.0 * math.pi * t_r / L
            f = jnp.linspace(0.0001, bands - 1.0, bands)[None, None]
            zc = jnp.exp(-1j * f * w)
            z = jnp.concatenate([t, zc.real, zc.imag], axis=-1)
            return (z.astype(jnp.float32), t.astype(jnp.float32))

        def _implicit_filter(z, w1, b1, w2, b2, w3, b3, wo, freq, t, deltas):
            h = jnp.sin(freq * (z @ w1 + b1))
            h = jnp.sin(freq * (h @ w2 + b2))
            h = jnp.sin(freq * (h @ w3 + b3))
            h = h @ wo
            decay = jnp.exp(-t * jnp.abs(deltas))
            return h * decay
        key = jax.random.key(seed)
        ks = jax.random.split(key, 24)
        z, _ = _pos_emb(SEQ, EMB)

        def lin(k, fan_in, fan_out):
            return jax.random.normal(k, (fan_in, fan_out), jnp.float32) / np.sqrt(fan_in)
        inp = {'x': jax.random.normal(ks[0], (B, D_MODEL, SEQ, SEQ), jnp.float32), 'z': z, 'Xw1': lin(ks[1], EMB, ORDER), 'Xb1': jax.random.normal(ks[2], (ORDER,), jnp.float32) * 0.02, 'Xw2': lin(ks[3], ORDER, ORDER), 'Xb2': jax.random.normal(ks[4], (ORDER,), jnp.float32) * 0.02, 'Xw3': lin(ks[5], ORDER, ORDER), 'Xb3': jax.random.normal(ks[6], (ORDER,), jnp.float32) * 0.02, 'Xwo': lin(ks[7], ORDER, D_MODEL), 'Xfreq': jnp.ones((1, ORDER), jnp.float32), 'Yw1': lin(ks[8], EMB, ORDER), 'Yb1': jax.random.normal(ks[9], (ORDER,), jnp.float32) * 0.02, 'Yw2': lin(ks[10], ORDER, ORDER), 'Yb2': jax.random.normal(ks[11], (ORDER,), jnp.float32) * 0.02, 'Yw3': lin(ks[12], ORDER, ORDER), 'Yb3': jax.random.normal(ks[13], (ORDER,), jnp.float32) * 0.02, 'Ywo': lin(ks[14], ORDER, D_MODEL), 'Yfreq': jnp.ones((1, ORDER), jnp.float32), 'bias': jax.random.normal(ks[15], (D_MODEL,), jnp.float32), 'L': SEQ}
        return inp
    _L0_conv_all = _L0_conv_setup()
    _L0_conv_in = {k: v for k, v in _L0_conv_all.items() if k in ('z', 'Xw1', 'Xb1', 'Xw2', 'Xb2', 'Xw3', 'Xb3', 'Xwo', 'Xfreq', 'Yw1', 'Yb1', 'Yw2', 'Yb2', 'Yw3', 'Yb3', 'Ywo', 'Yfreq', 'bias', )}
    del _L0_conv_all

    def _L1_conv_setup():
        import jax, jax.numpy as jnp
        import numpy as np
        BN_EPS = 1e-05
        key = jax.random.key(seed)
        k1, k2 = jax.random.split(key)
        B, P, S, D = (8, 64, 256, 256)
        x = jax.random.normal(k1, (B, P, S, D), dtype=jnp.float32)
        std = np.sqrt(2.0 / (S * S)).astype(np.float32)
        weights = jax.random.normal(k2, (P, S, S), dtype=jnp.float32) * std
        gamma = jnp.ones((P,), dtype=jnp.float32)
        beta = jnp.zeros((P,), dtype=jnp.float32)
        return {'x': x, 'weights': weights, 'gamma': gamma, 'beta': beta}
    _L1_conv_all = _L1_conv_setup()
    _L1_conv_in = {k: v for k, v in _L1_conv_all.items() if k in ('weights', 'gamma', 'beta', )}
    del _L1_conv_all

    return {
        "x": x,
        "L0_conv_z": _L0_conv_in["z"],
        "L0_conv_Xw1": _L0_conv_in["Xw1"],
        "L0_conv_Xb1": _L0_conv_in["Xb1"],
        "L0_conv_Xw2": _L0_conv_in["Xw2"],
        "L0_conv_Xb2": _L0_conv_in["Xb2"],
        "L0_conv_Xw3": _L0_conv_in["Xw3"],
        "L0_conv_Xb3": _L0_conv_in["Xb3"],
        "L0_conv_Xwo": _L0_conv_in["Xwo"],
        "L0_conv_Xfreq": _L0_conv_in["Xfreq"],
        "L0_conv_Yw1": _L0_conv_in["Yw1"],
        "L0_conv_Yb1": _L0_conv_in["Yb1"],
        "L0_conv_Yw2": _L0_conv_in["Yw2"],
        "L0_conv_Yb2": _L0_conv_in["Yb2"],
        "L0_conv_Yw3": _L0_conv_in["Yw3"],
        "L0_conv_Yb3": _L0_conv_in["Yb3"],
        "L0_conv_Ywo": _L0_conv_in["Ywo"],
        "L0_conv_Yfreq": _L0_conv_in["Yfreq"],
        "L0_conv_bias": _L0_conv_in["bias"],
        "L1_conv_weights": _L1_conv_in["weights"],
        "L1_conv_gamma": _L1_conv_in["gamma"],
        "L1_conv_beta": _L1_conv_in["beta"],
    }

def reference(x, L0_conv_z, L0_conv_Xw1, L0_conv_Xb1, L0_conv_Xw2, L0_conv_Xb2, L0_conv_Xw3, L0_conv_Xb3, L0_conv_Xwo, L0_conv_Xfreq, L0_conv_Yw1, L0_conv_Yb1, L0_conv_Yw2, L0_conv_Yb2, L0_conv_Yw3, L0_conv_Yb3, L0_conv_Ywo, L0_conv_Yfreq, L0_conv_bias, L1_conv_weights, L1_conv_gamma, L1_conv_beta):
    import jax
    import jax.numpy as jnp
    def _L0_conv_ref(x, z, Xw1, Xb1, Xw2, Xb2, Xw3, Xb3, Xwo, Xfreq, Yw1, Yb1, Yw2, Yb2, Yw3, Yb3, Ywo, Yfreq, bias, L):
        import jax, jax.numpy as jnp
        import numpy as np
        import math
        B, D_MODEL, EMB, ORDER, SEQ = (4, 64, 33, 64, 256)
        TARGET, FAST_PCT, SLOW_PCT = (0.01, 0.3, 1.5)

        def _pos_emb(L, emb_dim):
            t = jnp.linspace(0.0, 1.0, L)[None, :, None]
            bands = (emb_dim - 1) // 2
            t_r = jnp.linspace(0.0, L - 1.0, L)[None, :, None]
            w = 2.0 * math.pi * t_r / L
            f = jnp.linspace(0.0001, bands - 1.0, bands)[None, None]
            zc = jnp.exp(-1j * f * w)
            z = jnp.concatenate([t, zc.real, zc.imag], axis=-1)
            return (z.astype(jnp.float32), t.astype(jnp.float32))

        def _implicit_filter(z, w1, b1, w2, b2, w3, b3, wo, freq, t, deltas):
            h = jnp.sin(freq * (z @ w1 + b1))
            h = jnp.sin(freq * (h @ w2 + b2))
            h = jnp.sin(freq * (h @ w3 + b3))
            h = h @ wo
            decay = jnp.exp(-t * jnp.abs(deltas))
            return h * decay
        d_model = x.shape[1]
        t = jnp.linspace(0.0, 1.0, L)[None, :, None].astype(jnp.float32)
        max_dec = math.log(TARGET) / FAST_PCT
        min_dec = math.log(TARGET) / SLOW_PCT
        deltas = jnp.linspace(min_dec, max_dec, d_model)[None, None].astype(jnp.float32)
        hx = _implicit_filter(z, Xw1, Xb1, Xw2, Xb2, Xw3, Xb3, Xwo, Xfreq, t, deltas)
        hy = _implicit_filter(z, Yw1, Yb1, Yw2, Yb2, Yw3, Yb3, Ywo, Yfreq, t, deltas)
        k = jnp.einsum('ijk,imk->ijmk', hx, hy)[0]
        k = jnp.transpose(k, (2, 0, 1))
        fft_size = 2 * L
        k_f = jnp.fft.rfft2(k, s=(fft_size, fft_size)) / fft_size
        u_f = jnp.fft.rfft2(x.astype(jnp.float32), s=(fft_size, fft_size))
        y = jnp.fft.irfft2(u_f * k_f, s=(fft_size, fft_size))[..., :L, :L]
        out = y + x * bias[:, None, None]
        return out.astype(x.dtype)

    def _L1_conv_ref(x, weights, gamma, beta):
        import jax, jax.numpy as jnp
        import numpy as np
        BN_EPS = 1e-05
        D = x.shape[-1]
        inv_dim = 1.0 / jnp.sqrt(jnp.asarray(D, dtype=x.dtype))
        scores = jnp.einsum('bpsd,bptd->bpst', x, x) * inv_dim
        red = jnp.sum(scores * weights[None], axis=-1, keepdims=True)
        y = x + red
        mean = jnp.mean(y, axis=(0, 2, 3), keepdims=True)
        var = jnp.var(y, axis=(0, 2, 3), keepdims=True)
        y_hat = (y - mean) * jax.lax.rsqrt(var + BN_EPS)
        return y_hat * gamma[None, :, None, None] + beta[None, :, None, None]

    def _gn(v, G=32, eps=1e-5):
        B_, H_, W_, C_ = v.shape
        g = v.reshape(B_, H_, W_, G, C_ // G)
        m = jnp.mean(g, axis=(1, 2, 4), keepdims=True)
        s = jnp.var(g, axis=(1, 2, 4), keepdims=True)
        return ((g - m) / jnp.sqrt(s + eps)).reshape(v.shape)

    def _ln_c(v, eps=1e-6):
        m = jnp.mean(v, axis=-1, keepdims=True)
        s = jnp.var(v, axis=-1, keepdims=True)
        return (v - m) / jnp.sqrt(s + eps)

    def _ln_t(v, eps=1e-5):
        m = jnp.mean(v, axis=-1, keepdims=True)
        s = jnp.var(v, axis=-1, keepdims=True)
        return (v - m) / jnp.sqrt(s + eps)

    def _to_tokens(v):
        B_, H_, W_, C_ = v.shape
        return v.reshape(B_, H_ * W_, C_)
    def _from_tokens(t, like):
        return t.reshape(like.shape)

    x = _L0_conv_ref(x, L0_conv_z, L0_conv_Xw1, L0_conv_Xb1, L0_conv_Xw2, L0_conv_Xb2, L0_conv_Xw3, L0_conv_Xb3, L0_conv_Xwo, L0_conv_Xfreq, L0_conv_Yw1, L0_conv_Yb1, L0_conv_Yw2, L0_conv_Yb2, L0_conv_Yw3, L0_conv_Yb3, L0_conv_Ywo, L0_conv_Yfreq, L0_conv_bias, 256)
    x = _L1_conv_ref(x, L1_conv_weights, L1_conv_gamma, L1_conv_beta)
    return x


_drawn_inputs = setup_inputs


def setup_inputs(seed=0):
    import zlib

    import numpy as np

    out = dict(_drawn_inputs(seed))
    spreads = {'L0_conv_Xfreq': (1.0, 0.6),
     'L0_conv_Yfreq': (1.0, 0.6),
     'L1_conv_gamma': (1.0, 0.2),
     'L1_conv_beta': (0.0, 0.1)}
    factors = {'L0_conv_Xb1': 8.0,
     'L0_conv_Xb2': 8.0,
     'L0_conv_Xb3': 8.0,
     'L0_conv_Yb1': 8.0,
     'L0_conv_Yb2': 8.0,
     'L0_conv_Yb3': 8.0}
    for name, (base, spread) in spreads.items():
        noise = np.random.default_rng([zlib.crc32(name.encode()), seed]).standard_normal(out[name].shape)
        drawn = base * np.exp(spread * noise) if base else spread * noise
        out[name] = jnp.asarray(drawn.astype(out[name].dtype))
    for name, factor in factors.items():
        out[name] = (out[name] * factor).astype(out[name].dtype)
    return out
```

```python
import math
from contextlib import ExitStack

import concourse.bass as bass
import numpy as np
from concourse import mybir

F32 = mybir.dt.float32
F32R = mybir.dt.float32r
ALU = mybir.AluOpType
ACT = mybir.ActivationFunctionType

P = 128
BLOCKS = 2
SIDE = P * BLOCKS
EMB = 33
ORDER = 64
PAD = P + SIDE
BN_EPS = 1e-5

COL_W2, COL_W3, COL_WO = 0, P, 2 * P
COL_BIAS, COL_FREQ = 3 * P, 3 * P + 3
COL_DECAY = 3 * P + 4
COL_CHAN = COL_DECAY + SIDE

TWO_PI_PARTS = (6.28125, 0.0019350051879882812, 3.019916050561733e-07)
ROUND_MAGIC = 1.5 * 2.0 ** 23
PI_BELOW = 3.1415925

UNROLL = 8
LOAD_AHEAD = 4
LAG_U, LAG_Z, LAG_RED = 1, 2, 3
LAG_STAT, LAG_NORM = 5, 6


class Step:

    def __init__(self, body, place):
        self.body, self.place = body, place

    def static(self):
        return isinstance(self.body, int)

    def number(self, offset=0):
        return self.body * UNROLL + (self.place + offset)

    def channel(self, offset=0):
        return self.body * (UNROLL // 2) + (self.place // 2 + offset)

    def trail(self, lag):
        return Step(self.body, self.place - lag)

    def first_of_channel(self):
        return self.place % 2 == 0

    def half(self):
        return self.place % 2

    def slot(self, n):
        return self.place % n

    def ring(self, n):
        return self.place // 2 % n

    def turn(self, n):
        return self.body * (UNROLL // (2 * n)) + (self.place // 2 // n + 1)


def run_steps(engine, pairs, fill, last_lag, stage):
    for s in range(fill):
        stage(Step(s // UNROLL, s % UNROLL))
    with engine.Fori(fill // UNROLL, pairs // UNROLL) as body:
        for place in range(UNROLL):
            stage(Step(body, place))
    for s in range(pairs, pairs + last_lag + 1):
        stage(Step(s // UNROLL, s % UNROLL))


def build(nc, x, wt, zt, w1, params, out):
    CH, IMGS = x.shape[0], x.shape[2]
    PAIR = IMGS // 2
    PAIRS = CH * 2
    assert IMGS == 4 and PAIRS % UNROLL == 0
    GROUPS = IMGS * BLOCKS
    XR = 4
    NPARAM = params.shape[1]

    def active(st):
        return not st.static() or 0 <= st.number() < PAIRS

    def starts(st):
        return st.first_of_channel() and active(st)

    def wait(eng, sem, st, offset):
        if not st.static() or st.number(offset) > 0:
            eng.wait_ge(sem, st.number(offset))

    def wait_chan(eng, sem, st, offset):
        if not st.static() or st.channel(offset) > 0:
            eng.wait_ge(sem, st.channel(offset))

    with ExitStack() as ctx:
        def sb(name, shape, dt=F32):
            return ctx.enter_context(nc.sbuf_tensor(name, shape, dt))

        def ps(name, shape):
            return ctx.enter_context(nc.psum_tensor(name, shape, F32))

        def sem(name):
            return ctx.enter_context(nc.semaphore(name))

        pad_dram = nc.dram_tensor("filters_padded", [CH, 2, 2, PAD], F32, kind="Internal")

        par = sb("par", [P, NPARAM])
        zt_sb = sb("zt_sb", [EMB, SIDE])
        w1_sb = sb("w1_sb", [EMB, P])
        arg = sb("arg", [P, SIDE])
        turns = sb("turns", [P, SIDE])
        hid = sb("hid", [P, SIDE])
        filt = sb("filt", [P, 2, PAD], F32R)
        ones = sb("ones", [P, P])
        minus_half = sb("minus_half", [P, 1])

        x_sb = sb("x_sb", [P, XR, IMGS, BLOCKS, SIDE])
        xh = sb("xh", [P, 4, PAIR, BLOCKS, SIDE], F32R)
        xl = sb("xl", [P, 4, PAIR, BLOCKS, SIDE], F32R)
        toep = sb("toep", [P, XR, 2, 2, SIDE], F32R)
        uh = sb("uh", [P, 2, PAIR, BLOCKS, SIDE], F32R)
        ul = sb("ul", [P, 2, PAIR, BLOCKS, SIDE], F32R)
        z_sb = sb("z_sb", [P, XR, IMGS, BLOCKS, SIDE])
        zh = sb("zh", [P, 2, PAIR, BLOCKS, SIDE], F32R)
        zl = sb("zl", [P, 2, PAIR, BLOCKS, SIDE], F32R)
        w_sb = sb("w_sb", [P, 2, BLOCKS, SIDE])
        wh = sb("wh", [P, 2, BLOCKS, SIDE], F32R)
        wl = sb("wl", [P, 2, BLOCKS, SIDE], F32R)
        products = sb("products", [P, 2, PAIR, BLOCKS, SIDE], mybir.dt.bfloat16)
        red = sb("red", [P, XR, IMGS, BLOCKS])
        stat = sb("stat", [P, XR, GROUPS, 6])
        mv = sb("mv", [P, XR, 2])
        dev = sb("dev", [P, XR, 1])
        spread = sb("spread", [P, XR, 1])
        mean = sb("mean", [P, XR, 1])
        veps = sb("veps", [P, XR, 1])
        rstd = sb("rstd", [P, XR, 1])
        gain = sb("gain", [P, XR, 1])
        spacer = sb("spacer", [P, 1])
        centred = sb("centred", [P, XR, GROUPS])
        shift0 = sb("shift0", [P, XR, GROUPS])
        shift = sb("shift", [P, XR, GROUPS])

        ps_u = ps("ps_u", [P, PAIR, BLOCKS, SIDE])
        ps_z = ps("ps_z", [P, PAIR, BLOCKS, SIDE])
        ps_c = ps("ps_c", [P, BLOCKS, PAIR, SIDE])
        ps_mean = ps("ps_mean", [P, 512])
        ps_var = ps("ps_var", [P, 512])

        params_landed = sem("params_landed")
        const_ready = sem("const_ready")
        layer_done = sem("layer_done")
        reduce_step = sem("reduce_step")
        arg_ready = sem("arg_ready")
        hid_ready = sem("hid_ready")
        filt_ready = sem("filt_ready")
        filt_stored = sem("filt_stored")
        x_landed = [sem(f"x_landed{i}") for i in range(XR)]
        t_landed = [sem(f"t_landed{i}") for i in range(XR)]
        w_landed = [sem(f"w_landed{i}") for i in range(2)]
        xh_ready = sem("xh_ready")
        xl_ready = sem("xl_ready")
        wh_ready = sem("wh_ready")
        wl_ready = sem("wl_ready")
        u_done = sem("u_done")
        uh_ready = sem("uh_ready")
        ul_ready = sem("ul_ready")
        y_done = sem("y_done")
        z_ready = sem("z_ready")
        zh_ready = sem("zh_ready")
        zl_ready = sem("zl_ready")
        c_done = sem("c_done")
        bn_ready = sem("bn_ready")
        red_ready = sem("red_ready")
        shifted = sem("shifted")
        mv_ready = sem("mv_ready")
        mean_done = sem("mean_done")
        dev_ready = sem("dev_ready")
        spread_ready = sem("spread_ready")
        var_done = sem("var_done")
        veps_ready = sem("veps_ready")
        rstd_ready = sem("rstd_ready")
        gain_ready = sem("gain_ready")
        centred_ready = sem("centred_ready")
        shift0_ready = sem("shift0_ready")
        shift_ready = sem("shift_ready")
        norm_done = sem("norm_done")
        stored = [sem(f"stored{i}") for i in range(XR)]

        def chan_value(kind, st):
            return par[:, bass.ds(st.channel(COL_CHAN + kind * CH), 1)]

        block = ctx.enter_context(nc.Block())

        @block.sync
        def _(sp):
            sp.dma_start(zt_sb[:, :], zt).then_inc(params_landed, 16)
            sp.dma_start(w1_sb[:, :], w1).then_inc(params_landed, 16)
            sp.dma_start(par[:, :], params).then_inc(params_landed, 16)

            def load_x(m, slot):
                sp.dma_start(x_sb[:, slot, :, :, :].rearrange("p b k w -> p (b k w)"),
                             x[m, :, :, :, :].rearrange("p b k w -> p (b k w)"))\
                    .then_inc(x_landed[slot], 16)

            def load_w(m, slot):
                sp.dma_start(w_sb[:, slot % 2, :, :].rearrange("p k w -> p (k w)"),
                             wt[m, :, :, :].rearrange("p k w -> p (k w)"))\
                    .then_inc(w_landed[slot % 2], 16)

            def load_toeplitz(m, slot):
                src = bass.AP(pad_dram, m * (4 * PAD) + 1, [[1, P], [PAD, 4], [1, SIDE]])
                sp.dma_start(toep[:, slot, :, :, :].bitcast(F32).rearrange("p f q a -> p (f q) a"), src)\
                    .then_inc(t_landed[slot], 16)

            for m in range(2):
                load_x(m, m)
                load_w(m, m)
            sp.wait_ge(filt_ready, 2)
            for f in range(2):
                sp.dma_start(pad_dram[:, f, :, :].rearrange("c q n -> c (q n)"),
                             filt[f * CH:(f + 1) * CH, :, :].bitcast(F32).rearrange("c q n -> c (q n)"))\
                    .then_inc(filt_stored, 16)
            sp.wait_ge(filt_stored, 32)
            for m in range(2):
                load_toeplitz(m, m)

            def stage(st):
                if starts(st) and not (st.static() and st.channel() < 2):
                    m, slot = st.channel(), st.ring(XR)
                    wait(sp, z_ready, st, -2 * XR + 2)
                    load_x(m, slot)
                    wait(sp, y_done, st, -2 * XR + 2)
                    load_toeplitz(m, slot)
                    wait_chan(sp, wl_ready, st, -1)
                    load_w(m, slot)
                done = st.trail(LOAD_AHEAD + LAG_NORM + 2)
                if starts(done):
                    m, slot = done.channel(), done.ring(XR)
                    wait(sp, norm_done, done, 2)
                    sp.dma_start(out[m, :, :, :, :].rearrange("p b k w -> p (b k w)"),
                                 z_sb[:, slot, :, :, :].rearrange("p b k w -> p (b k w)"))\
                        .then_inc(stored[slot], 16)

            run_steps(sp, PAIRS, 2 * UNROLL, LOAD_AHEAD + LAG_NORM + 2, stage)
            for i in range(XR):
                sp.wait_ge(stored[i], 16 * (CH // XR))

        @block.gpsimd
        def _(pool):
            nc.gpsimd.memset(filt[:, :, 0:P].bitcast(F32), 0.0).then_inc(const_ready, 1)
            nc.gpsimd.memset(ones[:, :], 1.0 / P).then_inc(const_ready, 1)
            nc.gpsimd.memset(minus_half[:, :], -0.5).then_inc(const_ready, 1)
            pool.wait_ge(const_ready, 3)

            def stage(st):
                co = st.trail(LAG_NORM)
                if starts(co):
                    r = co.ring(XR)
                    wait_chan(pool, veps_ready, co, 1)
                    nc.gpsimd.tensor_tensor(rstd[:, r], veps[:, r], minus_half[:, :], ALU.pow)\
                        .then_inc(rstd_ready, 1)
                    wait_chan(pool, rstd_ready, co, 1)
                    nc.gpsimd.tensor_tensor(gain[:, r], rstd[:, r], chan_value(1, co), ALU.mult)\
                        .then_inc(gain_ready, 1)
                    wait_chan(pool, dev_ready, co, 1)
                    nc.gpsimd.tensor_tensor(centred[:, r], red[:, r].rearrange("p b k -> p (b k)"),
                                            mean[:, r].broadcast_to([P, GROUPS]), ALU.subtract)\
                        .then_inc(centred_ready, 1)
                    wait_chan(pool, gain_ready, co, 1)
                    wait_chan(pool, centred_ready, co, 1)
                    nc.gpsimd.tensor_tensor(shift0[:, r], centred[:, r],
                                            gain[:, r].broadcast_to([P, GROUPS]), ALU.mult)\
                        .then_inc(shift0_ready, 1)
                    wait_chan(pool, shift0_ready, co, 1)
                    nc.gpsimd.tensor_tensor(shift[:, r], shift0[:, r],
                                            chan_value(2, co).broadcast_to([P, GROUPS]), ALU.add)\
                        .then_inc(shift_ready, 1)

                if active(st):
                    wait(pool, xh_ready, st, 1)
                    r, h = st.ring(XR), st.half()
                    nc.gpsimd.tensor_tensor(xl[:, st.slot(4)], x_sb[:, r, PAIR * h:PAIR * (h + 1)],
                                            xh[:, st.slot(4)].bitcast(F32), ALU.subtract)\
                        .then_inc(xl_ready, 1)
                    if h == 0:
                        wait_chan(pool, wh_ready, st, 1)
                        nc.gpsimd.tensor_tensor(wl[:, r % 2], w_sb[:, r % 2], wh[:, r % 2].bitcast(F32),
                                                ALU.subtract).then_inc(wl_ready, 1)
                zs = st.trail(LAG_Z)
                if active(zs):
                    wait(pool, zh_ready, zs, 1)
                    r, h = zs.ring(XR), zs.half()
                    nc.gpsimd.tensor_tensor(zl[:, zs.slot(2)], z_sb[:, r, PAIR * h:PAIR * (h + 1)],
                                            zh[:, zs.slot(2)].bitcast(F32), ALU.subtract)\
                        .then_inc(zl_ready, 1)
            run_steps(pool, PAIRS, UNROLL, LAG_NORM + 1, stage)

        @block.scalar
        def _(act):
            for layer in range(3):
                act.wait_ge(arg_ready, layer + 1)
                nc.scalar.activation(hid[:, :], arg[:, :], ACT.Sin).then_inc(hid_ready, 1)

            def stage(st):
                if active(st):
                    r, h = st.ring(XR), st.half()
                    if h == 0:
                        act.wait_ge(x_landed[r], st.turn(XR) * 16)
                    wait(act, u_done, st, -3)
                    nc.scalar.activation(xh[:, st.slot(4)], x_sb[:, r, PAIR * h:PAIR * (h + 1)],
                                         ACT.Copy).then_inc(xh_ready, 1)
                    if h == 0:
                        act.wait_ge(w_landed[r % 2], st.turn(2) * 16)
                        wait(act, c_done, st, -2)
                        nc.scalar.activation(wh[:, r % 2], w_sb[:, r % 2], ACT.Copy).then_inc(wh_ready, 1)
                us = st.trail(LAG_U)
                if active(us):
                    wait(act, u_done, us, 1)
                    wait(act, y_done, us, -1)
                    nc.scalar.activation(uh[:, us.slot(2)], ps_u[:, :, :, :], ACT.Copy)\
                        .then_inc(uh_ready, 1)
                zs = st.trail(LAG_Z)
                if active(zs):
                    wait(act, z_ready, zs, 1)
                    wait(act, c_done, zs, -1)
                    r, h = zs.ring(XR), zs.half()
                    nc.scalar.activation(zh[:, zs.slot(2)], z_sb[:, r, PAIR * h:PAIR * (h + 1)],
                                         ACT.Copy).then_inc(zh_ready, 1)
                no = st.trail(LAG_NORM)
                if active(no):
                    if no.first_of_channel():
                        wait_chan(act, shift_ready, no, 1)
                    r, h = no.ring(XR), no.half()
                    for b in range(PAIR * h, PAIR * (h + 1)):
                        for k in range(BLOCKS):
                            g = b * BLOCKS + k
                            last = nc.scalar.activation(z_sb[:, r, b, k], z_sb[:, r, b, k], ACT.Identity,
                                                        bias=shift[:, r, g:g + 1], scale=gain[:, r])
                    last.then_inc(norm_done, 1)

            run_steps(act, PAIRS, UNROLL, LAG_NORM, stage)

        @block.tensor
        def _(pe):
            def mm(o, a, b, start, stop):
                return nc.tensor.matmul(o, a, b, start=start, stop=stop)

            pe.wait_ge(params_landed, 48)
            mm(ps_u[:, 0, 0, :], w1_sb[:, :], zt_sb[:, :], True, True).then_inc(layer_done, 1)
            for layer, col in enumerate((COL_W2, COL_W3, COL_WO)):
                pe.wait_ge(hid_ready, layer + 1)
                mm(ps_u[:, 0, 0, :], par[:, col:col + P], hid[:, :], True, True).then_inc(layer_done, 1)
            pe.wait_ge(filt_ready, 2)
            pe.wait_ge(const_ready, 3)

            def triangular(o, data_h, data_l, f, m_slot):
                for k in range(BLOCKS):
                    t_h, t_l = (toep[:, m_slot, f, q, 0:SIDE - P * k]
                                .rearrange("p (c j) -> p c j", j=P)[:, :, ::-1] for q in range(2))
                    mm(o[:, P * k:SIDE], data_h[k], t_h, k == 0, False)
                    mm(o[:, P * k:SIDE], data_h[k], t_l, False, False)
                    last = mm(o[:, P * k:SIDE], data_l[k], t_h, False, k == BLOCKS - 1)
                return last

            def stage(st):
                us = st.trail(LAG_U)
                if active(us):
                    if us.first_of_channel():
                        pe.wait_ge(t_landed[us.ring(XR)], us.turn(XR) * 16)
                    wait(pe, xl_ready, us, 1)
                    wait(pe, ul_ready, us, 0)
                    s = us.slot(4)
                    for b in range(PAIR):
                        for w in range(BLOCKS):
                            last = triangular(ps_u[:, b, w],
                                              [xh[:, s, b, k, P * w:P * (w + 1)] for k in range(BLOCKS)],
                                              [xl[:, s, b, k, P * w:P * (w + 1)] for k in range(BLOCKS)],
                                              0, us.ring(XR))
                    last.then_inc(u_done, 1)
                zs = st.trail(LAG_Z)
                if active(zs):
                    wait(pe, ul_ready, zs, 1)
                    wait(pe, z_ready, zs, 0)
                    s = zs.slot(2)
                    for b in range(PAIR):
                        for a in range(BLOCKS):
                            last = triangular(ps_z[:, b, a],
                                              [uh[:, s, b, k, P * a:P * (a + 1)] for k in range(BLOCKS)],
                                              [ul[:, s, b, k, P * a:P * (a + 1)] for k in range(BLOCKS)],
                                              1, zs.ring(XR))
                    last.then_inc(y_done, 1)
                ms = st.trail(LAG_STAT)
                if starts(ms):
                    wait_chan(pe, mv_ready, ms, 1)
                    mm(ps_mean[:, 0:1], ones[:, :], mv[:, ms.ring(XR), 0:1], True, True).then_inc(mean_done, 1)
                cs = st.trail(LAG_RED)
                if active(cs):
                    wait_chan(pe, wl_ready, cs, 1)
                    wait(pe, zl_ready, cs, 1)
                    wait(pe, red_ready, cs, 0)
                    s, w = cs.slot(2), cs.ring(2)
                    for a in range(BLOCKS):
                        for k in range(BLOCKS):
                            w_h, w_l = wh[:, w, k, P * a:P * (a + 1)], wl[:, w, k, P * a:P * (a + 1)]
                            mm(ps_c[:, a], w_h, zh[:, s, :, k], k == 0, False)
                            mm(ps_c[:, a], w_h, zl[:, s, :, k], False, False)
                            last = mm(ps_c[:, a], w_l, zh[:, s, :, k], False, k == BLOCKS - 1)
                    last.then_inc(c_done, 1)
                vs = st.trail(LAG_STAT)
                if starts(vs):
                    wait_chan(pe, spread_ready, vs, 1)
                    mm(ps_var[:, 0:1], ones[:, :], spread[:, vs.ring(XR)], True, True).then_inc(var_done, 1)

            run_steps(pe, PAIRS, UNROLL, LAG_STAT, stage)

        @block.vector
        def _(dve):
            dve.wait_ge(params_landed, 48)
            n = 0
            for layer in range(3):
                def own(ins):
                    nonlocal n
                    n += 1
                    ins.then_inc(reduce_step, 1)
                    dve.wait_ge(reduce_step, n)

                dve.wait_ge(layer_done, layer + 1)
                if layer > 0:
                    dve.wait_ge(hid_ready, layer)
                own(nc.vector.tensor_scalar(arg[:, :], ps_u[:, 0, 0, :],
                                            par[:, COL_BIAS + layer:COL_BIAS + layer + 1],
                                            par[:, COL_FREQ:COL_FREQ + 1], ALU.add, ALU.mult))
                own(nc.vector.tensor_scalar(turns[:, :], arg[:, :], 1.0 / (2.0 * math.pi), ROUND_MAGIC,
                                            ALU.mult, ALU.add))
                own(nc.vector.tensor_scalar(turns[:, :], turns[:, :], -ROUND_MAGIC, None, ALU.add))
                for part in TWO_PI_PARTS:
                    own(nc.vector.scalar_tensor_tensor(out=arg[:, :], in0=turns[:, :], scalar=-part,
                                                       in1=arg[:, :], op0=ALU.mult, op1=ALU.add))
                nc.vector.tensor_scalar(arg[:, :], arg[:, :], PI_BELOW, -PI_BELOW, ALU.min, ALU.max)\
                    .then_inc(arg_ready, 1)
            dve.wait_ge(layer_done, 4)
            own(nc.vector.tensor_tensor(turns[:, :], ps_u[:, 0, 0, :], par[:, COL_DECAY:COL_DECAY + SIDE],
                                        ALU.mult))
            dve.wait_ge(const_ready, 1)
            nc.vector.tensor_copy(filt[:, 0, P:PAD], turns[:, :]).then_inc(filt_ready, 1)
            dve.wait_ge(filt_ready, 1)
            nc.vector.tensor_tensor(filt[:, 1, P:PAD], turns[:, :], filt[:, 0, P:PAD].bitcast(F32),
                                    ALU.subtract).then_inc(filt_ready, 1)

            def stage(st):
                co = st.trail(LAG_NORM)
                if starts(co):
                    wait_chan(dve, var_done, co, 1)
                    nc.vector.tensor_scalar(veps[:, co.ring(XR)], ps_var[:, 0:1], BN_EPS, None, ALU.add)\
                        .then_inc(veps_ready, 1)

                ms = st.trail(LAG_STAT)
                if starts(ms):
                    r = ms.ring(XR)
                    wait(dve, red_ready, ms, 2)
                    wait(dve, bn_ready, ms, 2)
                    means = stat[:, r].rearrange("p g (h s) -> p g h s", h=2)[:, :, :, 1]
                    nc.vector.tensor_tensor(
                        means, means,
                        red[:, r].rearrange("p b k -> p (b k)").unsqueeze(2).broadcast_to([P, GROUPS, 2]),
                        ALU.add).then_inc(shifted, 1)
                    wait_chan(dve, shifted, ms, 1)
                    nc.vector.memset(spacer[:, :], 0.0)
                    nc.vector.bn_aggr(mv[:, r], stat[:, r].rearrange("p g s -> p (g s)"))\
                        .then_inc(mv_ready, 1)
                us = st.trail(LAG_U)
                if active(us):
                    wait(dve, uh_ready, us, 1)
                    nc.vector.tensor_tensor(ul[:, us.slot(2)], ps_u[:, :, :, :],
                                            uh[:, us.slot(2)].bitcast(F32), ALU.subtract)\
                        .then_inc(ul_ready, 1)
                zs = st.trail(LAG_Z)
                if active(zs):
                    r, h = zs.ring(XR), zs.half()
                    if h == 0:
                        if not zs.static() or zs.turn(XR) > 1:
                            dve.wait_ge(stored[r], (zs.turn(XR) - 1) * 16)
                    wait(dve, y_done, zs, 1)
                    nc.vector.scalar_tensor_tensor(
                        out=z_sb[:, r, PAIR * h:PAIR * (h + 1)].rearrange("p b k w -> p (b k w)"),
                        in0=x_sb[:, r, PAIR * h:PAIR * (h + 1)].rearrange("p b k w -> p (b k w)"),
                        scalar=chan_value(0, zs), in1=ps_z[:, :, :, :].rearrange("p b k w -> p (b k w)"),
                        op0=ALU.mult, op1=ALU.add).then_inc(z_ready, 1)
                vs = st.trail(LAG_STAT)
                if starts(vs):
                    r = vs.ring(XR)
                    wait_chan(dve, mean_done, vs, 1)
                    nc.vector.tensor_scalar(dev[:, r], mv[:, r, 0:1], ps_mean[:, 0:1], None, ALU.subtract)
                    nc.vector.tensor_copy(mean[:, r], ps_mean[:, 0:1]).then_inc(dev_ready, 1)
                    wait_chan(dve, dev_ready, vs, 1)
                    nc.vector.scalar_tensor_tensor(out=spread[:, r], in0=dev[:, r], scalar=dev[:, r],
                                                   in1=mv[:, r, 1:2], op0=ALU.mult, op1=ALU.add)\
                        .then_inc(spread_ready, 1)
                cs = st.trail(LAG_RED)
                if active(cs):
                    r, h = cs.ring(XR), cs.half()
                    wait(dve, c_done, cs, 1)
                    for b in range(PAIR):
                        for k in range(BLOCKS):
                            last = nc.vector.tensor_tensor_reduce(
                                products[:, cs.slot(2), b, k], z_sb[:, r, PAIR * h + b, k], ps_c[:, k, b],
                                1.0 / math.sqrt(SIDE), 0.0, ALU.mult, ALU.add,
                                red[:, r, PAIR * h + b, k:k + 1])
                    last.then_inc(red_ready, 1)
                if active(zs):
                    wait(dve, z_ready, zs, 1)
                    r, h = zs.ring(XR), zs.half()
                    for b in range(PAIR * h, PAIR * (h + 1)):
                        for k in range(BLOCKS):
                            last = nc.vector.bn_stats(stat[:, r, b * BLOCKS + k], z_sb[:, r, b, k])
                    last.then_inc(bn_ready, 1)

            run_steps(dve, PAIRS, 2 * UNROLL, LAG_NORM, stage)


def decay_rows(channels):
    t = np.linspace(0.0, 1.0, SIDE).astype(np.float32)
    deltas = np.linspace(math.log(0.01) / 1.5, math.log(0.01) / 0.3, channels).astype(np.float32)
    decay = np.exp((-t[None, :] * np.abs(deltas)[:, None]).astype(np.float32))
    return np.concatenate([decay, decay / np.float32(2 * SIDE)]).astype(np.float32)


def kernel(**inputs):
    import concourse.bacc as bacc
    from concourse.bass_utils import run_bass_kernel_spmd

    a = {k: np.asarray(v) for k, v in inputs.items()}
    x = a["x"]
    imgs, ch = x.shape[:2]

    def by_partition(images):
        n = images.shape[:-2]
        v = images.reshape(*n, BLOCKS, P, BLOCKS, P)[..., ::-1, :, ::-1]
        return v.reshape(*n, BLOCKS, P, SIDE).swapaxes(-3, -2)

    x_in = np.ascontiguousarray(by_partition(x).transpose(1, 2, 0, 3, 4))
    wt_in = np.ascontiguousarray(by_partition(a["L1_conv_weights"].transpose(0, 2, 1)))
    zt_in = np.ascontiguousarray(a["L0_conv_z"][0].T)
    w1_in = np.concatenate([a["L0_conv_Xw1"], a["L0_conv_Yw1"]], axis=1)
    params = np.zeros((P, COL_CHAN + 3 * ch), np.float32)
    for col, name in ((COL_W2, "w2"), (COL_W3, "w3"), (COL_WO, "wo")):
        params[0:ORDER, col:col + ORDER] = a["L0_conv_X" + name]
        params[ORDER:P, col + ORDER:col + P] = a["L0_conv_Y" + name]
    for i, name in enumerate(("b1", "b2", "b3", "freq")):
        params[0:ORDER, COL_BIAS + i] = a["L0_conv_X" + name].reshape(-1)
        params[ORDER:P, COL_BIAS + i] = a["L0_conv_Y" + name].reshape(-1)
    params[:, COL_DECAY:COL_DECAY + SIDE] = decay_rows(ch)
    for i, name in enumerate(("L0_conv_bias", "L1_conv_gamma", "L1_conv_beta")):
        params[:, COL_CHAN + i * ch:COL_CHAN + (i + 1) * ch] = a[name][None, :]

    arrays = {"x_in": x_in, "wt_in": wt_in, "zt_in": zt_in, "w1_in": w1_in, "params_in": params}
    nc = bacc.Bacc("TRN2", target_bir_lowering=False, num_devices=1)
    args = [nc.dram_tensor(n, v.shape, mybir.dt.from_np(v.dtype), kind="ExternalInput").ap()
            for n, v in arrays.items()]
    out = nc.dram_tensor("out", x_in.shape, F32, kind="ExternalOutput").ap()
    build(nc, *args, out)
    r = run_bass_kernel_spmd(nc, [arrays], core_ids=[0])
    y = r.results[0]["out"]
    y = y.transpose(2, 0, 3, 1, 4).reshape(imgs, ch, BLOCKS, P, BLOCKS, P)
    return np.ascontiguousarray(y[:, :, :, ::-1, :, ::-1]).reshape(x.shape)
```

```python
import math
from contextlib import ExitStack

import concourse.bass as bass
import numpy as np
from concourse import mybir

F32 = mybir.dt.float32
F32R = mybir.dt.float32r
ALU = mybir.AluOpType
ACT = mybir.ActivationFunctionType

P = 128
BLOCKS = 2
SIDE = P * BLOCKS
EMB = 33
ORDER = 64
PAD = P + SIDE
BN_EPS = 1e-5

COL_W2, COL_W3, COL_WO = 0, P, 2 * P
COL_BIAS, COL_FREQ = 3 * P, 3 * P + 3
COL_DECAY = 3 * P + 4
COL_CHAN = COL_DECAY + SIDE

ROUND_MAGIC = 1.5 * 2.0 ** 23
TWO_PI_BELOW = float(np.nextafter(np.float32(2.0 * math.pi), np.float32(0.0)))

UNROLL = 8
LOAD_AHEAD = 4
LAG_W, LAG_U, LAG_Z, LAG_RED = 2, 2, 3, 4
LAG_MEAN, LAG_VAR, LAG_NORM = 6, 7, 8
LAG_LOAD_W, LAG_LOAD_X, LAG_STORE = 2, 3, LOAD_AHEAD + LAG_NORM + 1


class Step:

    def __init__(self, body, place):
        self.body, self.place = body, place

    def static(self):
        return isinstance(self.body, int)

    def number(self, offset=0):
        return self.body * UNROLL + (self.place + offset)

    def channel(self, offset=0):
        return self.body * (UNROLL // 2) + (self.place // 2 + offset)

    def trail(self, lag):
        return Step(self.body, self.place - lag)

    def first_of_channel(self):
        return self.place % 2 == 0

    def half(self):
        return self.place % 2

    def slot(self, n):
        return self.place % n

    def ring(self, n):
        return self.place // 2 % n

    def turn(self, n):
        return self.body * (UNROLL // (2 * n)) + (self.place // 2 // n + 1)


def run_steps(engine, pairs, fill, last_lag, stage):
    for s in range(fill):
        stage(Step(s // UNROLL, s % UNROLL))
    with engine.Fori(fill // UNROLL, pairs // UNROLL) as body:
        for place in range(UNROLL):
            stage(Step(body, place))
    for s in range(pairs, pairs + last_lag + 1):
        stage(Step(s // UNROLL, s % UNROLL))


def build(nc, x, xt, wt, zt, w1, params, out):
    CH, IMGS = xt.shape[0], xt.shape[2]
    PAIR = IMGS // 2
    PAIRS = CH * 2
    assert IMGS == 4 and PAIRS % UNROLL == 0
    GROUPS = IMGS * BLOCKS
    XR = 4
    NPARAM = params.shape[1]

    def active(st):
        return not st.static() or 0 <= st.number() < PAIRS

    def starts(st):
        return st.first_of_channel() and active(st)

    def wait(eng, sem, st, offset):
        if not st.static() or st.number(offset) > 0:
            eng.wait_ge(sem, st.number(offset))

    def wait_chan(eng, sem, st, offset):
        if not st.static() or st.channel(offset) > 0:
            eng.wait_ge(sem, st.channel(offset))

    with ExitStack() as ctx:
        def sb(name, shape, dt=F32):
            return ctx.enter_context(nc.sbuf_tensor(name, shape, dt))

        def ps(name, shape):
            return ctx.enter_context(nc.psum_tensor(name, shape, F32))

        def sem(name):
            return ctx.enter_context(nc.semaphore(name))

        pad_dram = nc.dram_tensor("filters_padded", [CH, 5, PAD], F32, kind="Internal")

        par = sb("par", [P, NPARAM])
        zt_sb = sb("zt_sb", [EMB, SIDE])
        w1_sb = sb("w1_sb", [EMB, P])
        arg = sb("arg", [P, SIDE])
        turns = sb("turns", [P, SIDE])
        hid = sb("hid", [P, SIDE])
        part = sb("part", [P, SIDE])
        freq_turns = sb("freq_turns", [P, 1])
        filt = sb("filt", [P, 3, PAD])
        ones = sb("ones", [P, P])
        minus_half = sb("minus_half", [P, 1])

        xt_sb = sb("xt_sb", [P, XR, IMGS, BLOCKS, SIDE])
        x_sb = sb("x_sb", [P, 2, 2, BLOCKS, PAIR, SIDE])
        xh = sb("xh", [P, 4, PAIR, BLOCKS, SIDE], F32R)
        xl = sb("xl", [P, 4, PAIR, BLOCKS, SIDE], F32R)
        toep = sb("toep", [P, XR, 2, 2, SIDE], F32R)
        toep_whole = sb("toep_whole", [P, XR, P])
        uh = sb("uh", [P, 2, BLOCKS, PAIR, SIDE], F32R)
        ul = sb("ul", [P, 2, BLOCKS, PAIR, SIDE], F32R)
        z_sb = sb("z_sb", [P, XR, 2, BLOCKS, PAIR, SIDE])
        zh = sb("zh", [P, 2, BLOCKS, PAIR, SIDE], F32R)
        zl = sb("zl", [P, 2, BLOCKS, PAIR, SIDE], F32R)
        w_sb = sb("w_sb", [P, 2, BLOCKS, SIDE])
        wh = sb("wh", [P, 2, BLOCKS, SIDE], F32R)
        wl = sb("wl", [P, 2, BLOCKS, SIDE], F32R)
        products = sb("products", [P, 2, BLOCKS, PAIR, SIDE], mybir.dt.bfloat16)
        red = sb("red", [P, XR, GROUPS])
        stat = sb("stat", [P, XR, GROUPS, 6])
        mv = sb("mv", [P, XR, 2])
        dev = sb("dev", [P, XR, 1])
        spread = sb("spread", [P, XR, 1])
        mean = sb("mean", [P, XR, 1])
        veps = sb("veps", [P, XR, 1])
        rstd = sb("rstd", [P, XR, 1])
        gain = sb("gain", [P, XR, 1])
        spacer = sb("spacer", [P, 1])
        centred = sb("centred", [P, XR, GROUPS])
        shift0 = sb("shift0", [P, XR, GROUPS])
        shift = sb("shift", [P, XR, GROUPS])

        ps_u = ps("ps_u", [P, BLOCKS, PAIR, SIDE])
        ps_z = ps("ps_z", [P, BLOCKS, PAIR, SIDE])
        ps_c = ps("ps_c", [P, BLOCKS, PAIR, SIDE])
        ps_mean = ps("ps_mean", [P, 512])
        ps_var = ps("ps_var", [P, 512])

        params_landed = sem("params_landed")
        const_ready = sem("const_ready")
        layer_done = sem("layer_done")
        reduced = sem("reduced")
        hid_ready = sem("hid_ready")
        filt_ready = sem("filt_ready")
        filt_stored = sem("filt_stored")
        xt_landed = [sem(f"xt_landed{i}") for i in range(XR)]
        x_landed = [sem(f"x_landed{i}") for i in range(2)]
        t_landed = [sem(f"t_landed{i}") for i in range(XR)]
        w_landed = [sem(f"w_landed{i}") for i in range(2)]
        xh_ready = sem("xh_ready")
        xl_ready = sem("xl_ready")
        wh_ready = sem("wh_ready")
        wl_ready = sem("wl_ready")
        u_done = sem("u_done")
        uh_ready = sem("uh_ready")
        ul_ready = sem("ul_ready")
        y_done = sem("y_done")
        z_ready = sem("z_ready")
        zh_ready = sem("zh_ready")
        zl_ready = sem("zl_ready")
        c_done = sem("c_done")
        bn_ready = sem("bn_ready")
        red_ready = sem("red_ready")
        shifted = sem("shifted")
        mv_ready = sem("mv_ready")
        mean_done = sem("mean_done")
        dev_ready = sem("dev_ready")
        spread_ready = sem("spread_ready")
        var_done = sem("var_done")
        veps_ready = sem("veps_ready")
        rstd_ready = sem("rstd_ready")
        gain_ready = sem("gain_ready")
        centred_ready = sem("centred_ready")
        shift0_ready = sem("shift0_ready")
        shift_ready = sem("shift_ready")
        norm_done = sem("norm_done")
        stored = [[sem(f"stored{i}_{h}") for h in range(2)] for i in range(XR)]

        def chan_value(kind, st):
            return par[:, bass.ds(st.channel(COL_CHAN + kind * CH), 1)]

        block = ctx.enter_context(nc.Block())

        @block.sync
        def _(sp):
            sp.dma_start(zt_sb[:, :], zt).then_inc(params_landed, 16)
            sp.dma_start(w1_sb[:, :], w1).then_inc(params_landed, 16)
            sp.dma_start(par[:, :], params).then_inc(params_landed, 16)

            def load_xt(m, slot):
                sp.dma_start(xt_sb[:, slot, :, :, :].rearrange("p b k h -> p (b k h)"),
                             xt[m, :, :, :, :].rearrange("p b k h -> p (b k h)"))\
                    .then_inc(xt_landed[slot], 16)

            def load_x(m, slot):
                sp.dma_start(x_sb[:, slot, :, :, :, :].rearrange("p c k b w -> p (c k b w)"),
                             x[m, :, :, :, :, :].rearrange("p c k b w -> p (c k b w)"))\
                    .then_inc(x_landed[slot], 16)

            def load_w(m, slot):
                sp.dma_start(w_sb[:, slot, :, :].rearrange("p k w -> p (k w)"),
                             wt[m, :, :, :].rearrange("p k w -> p (k w)"))\
                    .then_inc(w_landed[slot], 16)

            def load_toeplitz(m, slot):
                src = bass.AP(pad_dram, m * (5 * PAD) + 1, [[1, P], [PAD, 4], [1, SIDE]])
                sp.dma_start(toep[:, slot, :, :, :].bitcast(F32).rearrange("p f q a -> p (f q) a"), src)\
                    .then_inc(t_landed[slot], 16)
                src = bass.AP(pad_dram, m * (5 * PAD) + (4 * PAD + 1), [[1, P], [1, P]])
                sp.dma_start(toep_whole[:, slot, :], src).then_inc(t_landed[slot], 16)

            load_xt(0, 0)
            load_w(0, 0)
            load_xt(1, 1)
            sp.wait_ge(filt_ready, 3)
            for f in range(2):
                sp.dma_start(pad_dram[:, 2 * f:2 + 3 * f, :].rearrange("c q n -> c (q n)"),
                             filt[f * CH:(f + 1) * CH, 0:2 + f, :].rearrange("c q n -> c (q n)"))\
                    .then_inc(filt_stored, 16)
            sp.wait_ge(filt_stored, 32)

            def stage(st):
                done = st.trail(LAG_STORE)
                if active(done):
                    m, slot, h = done.channel(), done.ring(XR), done.half()
                    wait(sp, norm_done, done, 1)
                    sp.dma_start(out[m, :, h, :, :, :].rearrange("p k b w -> p (k b w)"),
                                 z_sb[:, slot, h, :, :, :].rearrange("p k b w -> p (k b w)"))\
                        .then_inc(stored[slot][h], 16)
                if starts(st):
                    m, slot = st.channel(), st.ring(XR)
                    wait(sp, y_done, st, -2 * XR + 2)
                    load_toeplitz(m, slot)
                    if not (st.static() and m < 2):
                        load_xt(m, slot)
                ws = st.trail(LAG_LOAD_W)
                if starts(ws) and not (ws.static() and ws.channel() < 1):
                    wait_chan(sp, wl_ready, ws, -1)
                    load_w(ws.channel(), ws.ring(2))
                xs = st.trail(LAG_LOAD_X)
                if starts(xs):
                    wait(sp, z_ready, xs, -2)
                    load_x(xs.channel(), xs.ring(2))

            run_steps(sp, PAIRS, 2 * UNROLL, LAG_STORE, stage)
            for i in range(XR):
                for h in range(2):
                    sp.wait_ge(stored[i][h], 16 * (CH // XR))

        @block.gpsimd
        def _(pool):
            nc.gpsimd.memset(filt[:, :, 0:P], 0.0).then_inc(const_ready, 1)
            nc.gpsimd.memset(ones[:, :], 1.0 / P).then_inc(const_ready, 1)
            nc.gpsimd.memset(minus_half[:, :], -0.5).then_inc(const_ready, 1)
            pool.wait_ge(const_ready, 3)

            def stage(st):
                co = st.trail(LAG_NORM)
                if starts(co):
                    r = co.ring(XR)
                    wait_chan(pool, veps_ready, co, 1)
                    nc.gpsimd.tensor_tensor(rstd[:, r], veps[:, r], minus_half[:, :], ALU.pow)\
                        .then_inc(rstd_ready, 1)
                    wait_chan(pool, rstd_ready, co, 1)
                    nc.gpsimd.tensor_tensor(gain[:, r], rstd[:, r], chan_value(1, co), ALU.mult)\
                        .then_inc(gain_ready, 1)
                    wait_chan(pool, dev_ready, co, 1)
                    nc.gpsimd.tensor_tensor(centred[:, r], red[:, r],
                                            mean[:, r].broadcast_to([P, GROUPS]), ALU.subtract)\
                        .then_inc(centred_ready, 1)
                    wait_chan(pool, gain_ready, co, 1)
                    wait_chan(pool, centred_ready, co, 1)
                    nc.gpsimd.tensor_tensor(shift0[:, r], centred[:, r],
                                            gain[:, r].broadcast_to([P, GROUPS]), ALU.mult)\
                        .then_inc(shift0_ready, 1)
                    wait_chan(pool, shift0_ready, co, 1)
                    nc.gpsimd.tensor_tensor(shift[:, r], shift0[:, r],
                                            chan_value(2, co).broadcast_to([P, GROUPS]), ALU.add)\
                        .then_inc(shift_ready, 1)

                if active(st):
                    wait(pool, xh_ready, st, 1)
                    r, h = st.ring(XR), st.half()
                    nc.gpsimd.tensor_tensor(xl[:, st.slot(4)], xt_sb[:, r, PAIR * h:PAIR * (h + 1)],
                                            xh[:, st.slot(4)].bitcast(F32), ALU.subtract)\
                        .then_inc(xl_ready, 1)
                ws = st.trail(LAG_W)
                if starts(ws):
                    r = ws.ring(2)
                    wait_chan(pool, wh_ready, ws, 1)
                    nc.gpsimd.tensor_tensor(wl[:, r], w_sb[:, r], wh[:, r].bitcast(F32),
                                            ALU.subtract).then_inc(wl_ready, 1)
                zs = st.trail(LAG_Z)
                if active(zs):
                    wait(pool, zh_ready, zs, 1)
                    r, h = zs.ring(XR), zs.half()
                    nc.gpsimd.tensor_tensor(zl[:, zs.slot(2)], z_sb[:, r, h],
                                            zh[:, zs.slot(2)].bitcast(F32), ALU.subtract)\
                        .then_inc(zl_ready, 1)
            run_steps(pool, PAIRS, UNROLL, LAG_NORM + 1, stage)

        @block.scalar
        def _(act):
            for layer in range(3):
                act.wait_ge(reduced, 3 * layer + 4)
                nc.scalar.activation(hid[:, :], part[:, :], ACT.Sin, scale=TWO_PI_BELOW)\
                    .then_inc(hid_ready, 1)

            def stage(st):
                if active(st):
                    r, h = st.ring(XR), st.half()
                    if h == 0:
                        act.wait_ge(xt_landed[r], st.turn(XR) * 16)
                    wait(act, u_done, st, -3)
                    nc.scalar.activation(xh[:, st.slot(4)], xt_sb[:, r, PAIR * h:PAIR * (h + 1)],
                                         ACT.Copy).then_inc(xh_ready, 1)
                ws = st.trail(LAG_W)
                if starts(ws):
                    r = ws.ring(2)
                    act.wait_ge(w_landed[r], ws.turn(2) * 16)
                    wait(act, c_done, ws, -2)
                    nc.scalar.activation(wh[:, r], w_sb[:, r], ACT.Copy).then_inc(wh_ready, 1)
                us = st.trail(LAG_U)
                if active(us):
                    wait(act, u_done, us, 1)
                    wait(act, y_done, us, -1)
                    nc.scalar.activation(uh[:, us.slot(2)], ps_u[:, :, :, :], ACT.Copy)\
                        .then_inc(uh_ready, 1)
                no = st.trail(LAG_NORM)
                if active(no):
                    if no.first_of_channel():
                        wait_chan(act, shift_ready, no, 1)
                    r, h = no.ring(XR), no.half()
                    for k in range(BLOCKS):
                        for b in range(PAIR):
                            g = (h * BLOCKS + k) * PAIR + b
                            last = nc.scalar.activation(z_sb[:, r, h, k, b], z_sb[:, r, h, k, b], ACT.Identity,
                                                        bias=shift[:, r, g:g + 1], scale=gain[:, r])
                    last.then_inc(norm_done, 1)
                zs = st.trail(LAG_Z)
                if active(zs):
                    wait(act, z_ready, zs, 1)
                    wait(act, c_done, zs, -1)
                    r, h = zs.ring(XR), zs.half()
                    nc.scalar.activation(zh[:, zs.slot(2)], z_sb[:, r, h],
                                         ACT.Copy).then_inc(zh_ready, 1)

            run_steps(act, PAIRS, UNROLL, LAG_NORM, stage)

        @block.tensor
        def _(pe):
            def mm(o, a, b, start, stop):
                return nc.tensor.matmul(o, a, b, start=start, stop=stop)

            pe.wait_ge(params_landed, 48)
            mm(ps_u[:, 0, 0, :], w1_sb[:, :], zt_sb[:, :], True, True).then_inc(layer_done, 1)
            for layer, col in enumerate((COL_W2, COL_W3, COL_WO)):
                pe.wait_ge(hid_ready, layer + 1)
                mm(ps_u[:, 0, 0, :], par[:, col:col + P], hid[:, :], True, True).then_inc(layer_done, 1)
            pe.wait_ge(filt_ready, 1)
            pe.wait_ge(const_ready, 3)

            def stage(st):
                us = st.trail(LAG_U)
                if active(us):
                    r = us.ring(XR)
                    if us.first_of_channel():
                        pe.wait_ge(t_landed[r], us.turn(XR) * 32)
                    wait(pe, xl_ready, us, 1)
                    wait(pe, ul_ready, us, 0)
                    s = us.slot(4)
                    for h in range(BLOCKS):
                        rows = slice(P * h, P * (h + 1))
                        for b in range(PAIR):
                            o = ps_u[:, h, b, :]
                            mm(o, xh[:, s, b, 0, rows], toep[:, r, 1, 0, :], True, False)
                            mm(o, xh[:, s, b, 0, rows], toep[:, r, 1, 1, :], False, False)
                            mm(o, xl[:, s, b, 0, rows], toep[:, r, 1, 0, :], False, False)
                            last = mm(o[:, P:SIDE], xt_sb[:, r, PAIR * us.half() + b, 1, rows],
                                      toep_whole[:, r, :], False, True)
                    last.then_inc(u_done, 1)
                zs = st.trail(LAG_Z)
                if active(zs):
                    wait(pe, ul_ready, zs, 1)
                    wait(pe, z_ready, zs, 0)
                    s, r = zs.slot(2), zs.ring(XR)
                    for a in range(BLOCKS):
                        for h in range(a + 1):
                            cols = slice(P * (a - h), P * (a - h + 1))
                            t_h, t_l = toep[:, r, 0, 0, cols], toep[:, r, 0, 1, cols]
                            mm(ps_z[:, a], t_h, uh[:, s, h], h == 0, False)
                            mm(ps_z[:, a], t_h, ul[:, s, h], False, False)
                            last = mm(ps_z[:, a], t_l, uh[:, s, h], False, h == a)
                    last.then_inc(y_done, 1)
                cs = st.trail(LAG_RED)
                if active(cs):
                    wait_chan(pe, wl_ready, cs, 1)
                    wait(pe, zl_ready, cs, 1)
                    wait(pe, red_ready, cs, 0)
                    s, w = cs.slot(2), cs.ring(2)
                    for a in range(BLOCKS):
                        for k in range(BLOCKS):
                            w_h, w_l = wh[:, w, k, P * a:P * (a + 1)], wl[:, w, k, P * a:P * (a + 1)]
                            mm(ps_c[:, a], w_h, zh[:, s, k], k == 0, False)
                            mm(ps_c[:, a], w_h, zl[:, s, k], False, False)
                            last = mm(ps_c[:, a], w_l, zh[:, s, k], False, k == BLOCKS - 1)
                    last.then_inc(c_done, 1)
                ms = st.trail(LAG_MEAN)
                if starts(ms):
                    wait_chan(pe, mv_ready, ms, 1)
                    mm(ps_mean[:, 0:1], ones[:, :], mv[:, ms.ring(XR), 0:1], True, True).then_inc(mean_done, 1)
                vs = st.trail(LAG_VAR)
                if starts(vs):
                    wait_chan(pe, spread_ready, vs, 1)
                    mm(ps_var[:, 0:1], ones[:, :], spread[:, vs.ring(XR)], True, True).then_inc(var_done, 1)

            run_steps(pe, PAIRS, UNROLL, LAG_VAR, stage)

        @block.vector
        def _(dve):
            dve.wait_ge(params_landed, 48)
            nc.vector.tensor_scalar(freq_turns[:, :], par[:, COL_FREQ:COL_FREQ + 1], 1.0 / (2.0 * math.pi),
                                    None, ALU.mult).then_inc(reduced, 1)
            for layer in range(3):
                dve.wait_ge(layer_done, layer + 1)
                dve.wait_ge(reduced, 3 * layer + 1)
                nc.vector.tensor_scalar(arg[:, :], ps_u[:, 0, 0, :],
                                        par[:, COL_BIAS + layer:COL_BIAS + layer + 1],
                                        freq_turns[:, 0:1], ALU.add, ALU.mult).then_inc(reduced, 1)
                dve.wait_ge(reduced, 3 * layer + 2)
                nc.vector.tensor_scalar(turns[:, :], arg[:, :], ROUND_MAGIC, ROUND_MAGIC,
                                        ALU.add, ALU.subtract).then_inc(reduced, 1)
                dve.wait_ge(reduced, 3 * layer + 3)
                if layer > 0:
                    dve.wait_ge(hid_ready, layer)
                nc.vector.tensor_tensor(part[:, :], arg[:, :], turns[:, :], ALU.subtract)\
                    .then_inc(reduced, 1)
            dve.wait_ge(layer_done, 4)
            dve.wait_ge(const_ready, 1)
            nc.vector.tensor_tensor(filt[:, 2, P:PAD], ps_u[:, 0, 0, :], par[:, COL_DECAY:COL_DECAY + SIDE],
                                    ALU.mult).then_inc(filt_ready, 1)
            dve.wait_ge(filt_ready, 1)
            nc.vector.tensor_copy(filt[:, 0, P:PAD].bitcast(F32R), filt[:, 2, P:PAD]).then_inc(filt_ready, 1)
            dve.wait_ge(filt_ready, 2)
            nc.vector.tensor_tensor(filt[:, 1, P:PAD].bitcast(F32R), filt[:, 2, P:PAD], filt[:, 0, P:PAD],
                                    ALU.subtract).then_inc(filt_ready, 1)

            def stage(st):
                co = st.trail(LAG_NORM)
                if starts(co):
                    wait_chan(dve, var_done, co, 1)
                    nc.vector.tensor_scalar(veps[:, co.ring(XR)], ps_var[:, 0:1], BN_EPS, None, ALU.add)\
                        .then_inc(veps_ready, 1)

                vs = st.trail(LAG_VAR)
                if starts(vs):
                    r = vs.ring(XR)
                    wait_chan(dve, mean_done, vs, 1)
                    nc.vector.tensor_scalar(dev[:, r], mv[:, r, 0:1], ps_mean[:, 0:1], None, ALU.subtract)
                    nc.vector.tensor_copy(mean[:, r], ps_mean[:, 0:1]).then_inc(dev_ready, 1)
                    wait_chan(dve, dev_ready, vs, 1)
                    nc.vector.scalar_tensor_tensor(out=spread[:, r], in0=dev[:, r], scalar=dev[:, r],
                                                   in1=mv[:, r, 1:2], op0=ALU.mult, op1=ALU.add)\
                        .then_inc(spread_ready, 1)
                ms = st.trail(LAG_MEAN)
                if starts(ms):
                    r = ms.ring(XR)
                    wait(dve, red_ready, ms, 2)
                    wait(dve, bn_ready, ms, 2)
                    means = stat[:, r].rearrange("p g (h s) -> p g h s", h=2)[:, :, :, 1]
                    nc.vector.tensor_tensor(
                        means, means,
                        red[:, r].unsqueeze(2).broadcast_to([P, GROUPS, 2]),
                        ALU.add).then_inc(shifted, 1)
                    wait_chan(dve, shifted, ms, 1)
                    nc.vector.memset(spacer[:, :], 0.0)
                    nc.vector.bn_aggr(mv[:, r], stat[:, r].rearrange("p g s -> p (g s)"))\
                        .then_inc(mv_ready, 1)
                us = st.trail(LAG_U)
                if active(us):
                    wait(dve, uh_ready, us, 1)
                    nc.vector.tensor_tensor(ul[:, us.slot(2)], ps_u[:, :, :, :],
                                            uh[:, us.slot(2)].bitcast(F32), ALU.subtract)\
                        .then_inc(ul_ready, 1)
                zs = st.trail(LAG_Z)
                if active(zs):
                    r, h = zs.ring(XR), zs.half()
                    if h == 0:
                        dve.wait_ge(x_landed[zs.ring(2)], zs.turn(2) * 16)
                    if not zs.static() or zs.turn(XR) > 1:
                        dve.wait_ge(stored[r][h], (zs.turn(XR) - 1) * 16)
                    wait(dve, y_done, zs, 1)
                    nc.vector.scalar_tensor_tensor(
                        out=z_sb[:, r, h].rearrange("p k b w -> p (k b w)"),
                        in0=x_sb[:, zs.ring(2), h].rearrange("p k b w -> p (k b w)"),
                        scalar=chan_value(0, zs), in1=ps_z[:, :, :, :].rearrange("p k b w -> p (k b w)"),
                        op0=ALU.mult, op1=ALU.add).then_inc(z_ready, 1)
                cs = st.trail(LAG_RED)
                if active(cs):
                    r, h = cs.ring(XR), cs.half()
                    wait(dve, c_done, cs, 1)
                    for k in range(BLOCKS):
                        for b in range(PAIR):
                            g = (h * BLOCKS + k) * PAIR + b
                            last = nc.vector.tensor_tensor_reduce(
                                products[:, cs.slot(2), k, b], z_sb[:, r, h, k, b], ps_c[:, k, b],
                                1.0 / math.sqrt(SIDE), 0.0, ALU.mult, ALU.add, red[:, r, g:g + 1])
                    last.then_inc(red_ready, 1)
                if active(zs):
                    wait(dve, z_ready, zs, 1)
                    r, h = zs.ring(XR), zs.half()
                    for k in range(BLOCKS):
                        for b in range(PAIR):
                            last = nc.vector.bn_stats(stat[:, r, (h * BLOCKS + k) * PAIR + b],
                                                      z_sb[:, r, h, k, b])
                    last.then_inc(bn_ready, 1)

            run_steps(dve, PAIRS, 2 * UNROLL, LAG_NORM, stage)


def decay_rows(channels):
    t = np.linspace(0.0, 1.0, SIDE).astype(np.float32)
    deltas = np.linspace(math.log(0.01) / 1.5, math.log(0.01) / 0.3, channels).astype(np.float32)
    decay = np.exp((-t[None, :] * np.abs(deltas)[:, None]).astype(np.float32))
    return np.concatenate([decay, decay / np.float32(2 * SIDE)]).astype(np.float32)


def kernel(**inputs):
    import concourse.bacc as bacc
    from concourse.bass_utils import run_bass_kernel_spmd

    a = {k: np.asarray(v) for k, v in inputs.items()}
    x = a["x"]
    imgs, ch = x.shape[:2]

    x_in = np.ascontiguousarray(
        x.reshape(2, imgs // 2, ch, BLOCKS, P, SIDE).transpose(2, 4, 0, 3, 1, 5))
    xt_in = np.ascontiguousarray(
        x.reshape(imgs, ch, BLOCKS, P, BLOCKS, P)[:, :, :, ::-1, :, ::-1].transpose(1, 5, 0, 4, 2, 3)
    ).reshape(ch, P, imgs, BLOCKS, SIDE)
    wt_in = np.ascontiguousarray(
        a["L1_conv_weights"].reshape(ch, SIDE, BLOCKS, P).transpose(0, 3, 2, 1))
    zt_in = np.ascontiguousarray(a["L0_conv_z"][0].T)
    w1_in = np.concatenate([a["L0_conv_Xw1"], a["L0_conv_Yw1"]], axis=1)
    params = np.zeros((P, COL_CHAN + 3 * ch), np.float32)
    for col, name in ((COL_W2, "w2"), (COL_W3, "w3"), (COL_WO, "wo")):
        params[0:ORDER, col:col + ORDER] = a["L0_conv_X" + name]
        params[ORDER:P, col + ORDER:col + P] = a["L0_conv_Y" + name]
    for i, name in enumerate(("b1", "b2", "b3", "freq")):
        params[0:ORDER, COL_BIAS + i] = a["L0_conv_X" + name].reshape(-1)
        params[ORDER:P, COL_BIAS + i] = a["L0_conv_Y" + name].reshape(-1)
    params[:, COL_DECAY:COL_DECAY + SIDE] = decay_rows(ch)
    for i, name in enumerate(("L0_conv_bias", "L1_conv_gamma", "L1_conv_beta")):
        params[:, COL_CHAN + i * ch:COL_CHAN + (i + 1) * ch] = a[name][None, :]

    arrays = {"x_in": x_in, "xt_in": xt_in, "wt_in": wt_in, "zt_in": zt_in, "w1_in": w1_in, "params_in": params}
    nc = bacc.Bacc("TRN2", target_bir_lowering=False, num_devices=1)
    args = [nc.dram_tensor(n, v.shape, mybir.dt.from_np(v.dtype), kind="ExternalInput").ap()
            for n, v in arrays.items()]
    out = nc.dram_tensor("out", x_in.shape, F32, kind="ExternalOutput").ap()
    build(nc, *args, out)
    r = run_bass_kernel_spmd(nc, [arrays], core_ids=[0])
    y = r.results[0]["out"]
    return np.ascontiguousarray(y.transpose(2, 4, 0, 3, 1, 5)).reshape(x.shape)
```

```python
import math
from contextlib import ExitStack

import concourse.bass as bass
import numpy as np
from concourse import mybir

F32 = mybir.dt.float32
F32R = mybir.dt.float32r
ALU = mybir.AluOpType
ACT = mybir.ActivationFunctionType

P = 128
BLOCKS = 2
SIDE = P * BLOCKS
EMB = 33
ORDER = 64
PAD = P + SIDE
BN_EPS = 1e-5

COL_ZT, COL_W1 = 0, SIDE
COL_BIAS, COL_FREQ = COL_W1 + P, COL_W1 + P + 3
COL_W2, COL_W3, COL_WO = (COL_FREQ + 1 + i * P for i in range(3))
COL_DECAY = COL_WO + P
COL_CHAN = COL_DECAY + SIDE

ROUND_MAGIC = 1.5 * 2.0 ** 23
TWO_PI_BELOW = float(np.nextafter(np.float32(2.0 * math.pi), np.float32(0.0)))

WARM_FIRST, WARM_LAYER, WARM_TOEPLITZ = 3, 3, 28

UNROLL = 8
LOAD_AHEAD = 4
LAG_T, LAG_W = 1, 2
LAG_U, LAG_Z, LAG_RED = 2, 3, 4
LAG_MEAN, LAG_SPREAD, LAG_NORM = 6, 7, 9
LAG_LOAD_XT, LAG_LOAD_T, LAG_LOAD_W, LAG_LOAD_X = 1, 3, 3, 5
LAG_STORE = LOAD_AHEAD + LAG_NORM + 1
END_STEPS = 1


class Step:

    def __init__(self, body, place):
        self.body, self.place = body, place

    def static(self):
        return isinstance(self.body, int)

    def number(self, offset=0):
        return self.body * UNROLL + (self.place + offset)

    def channel(self, offset=0):
        return self.body * (UNROLL // 2) + (self.place // 2 + offset)

    def trail(self, lag):
        return Step(self.body, self.place - lag)

    def first_of_channel(self):
        return self.place % 2 == 0

    def half(self):
        return self.place % 2

    def slot(self, n):
        return self.place % n

    def ring(self, n):
        return self.place // 2 % n

    def turn(self, n):
        return self.body * (UNROLL // (2 * n)) + (self.place // 2 // n + 1)


def run_steps(engine, pairs, fill, last_lag, stage):
    for s in range(fill):
        stage(Step(s // UNROLL, s % UNROLL))
    with engine.Fori(fill // UNROLL, pairs // UNROLL) as body:
        for place in range(UNROLL):
            stage(Step(body, place))
    for s in range(pairs, pairs + last_lag + 1):
        stage(Step(s // UNROLL, s % UNROLL))


def build(nc, x, xt, wt, params, out):
    CH, IMGS = xt.shape[0], xt.shape[2]
    PAIR = IMGS // 2
    PAIRS = CH * 2
    assert IMGS == 4 and PAIRS % UNROLL == 0
    GROUPS = IMGS * BLOCKS
    XR = 4
    NPARAM = params.shape[1]

    def active(st):
        return not st.static() or 0 <= st.number() < PAIRS

    def starts(st):
        return st.first_of_channel() and active(st)

    def ending(st, count):
        return st.static() and PAIRS - count <= st.number() < PAIRS

    def second_pair(st):
        return st.static() and st.number() == 1

    def wait(eng, sem, st, offset):
        if not st.static() or st.number(offset) > 0:
            eng.wait_ge(sem, st.number(offset))

    def wait_chan(eng, sem, st, offset):
        if not st.static() or st.channel(offset) > 0:
            eng.wait_ge(sem, st.channel(offset))

    with ExitStack() as ctx:
        def sb(name, shape, dt=F32):
            return ctx.enter_context(nc.sbuf_tensor(name, shape, dt))

        def ps(name, shape):
            return ctx.enter_context(nc.psum_tensor(name, shape, F32))

        def sem(name):
            return ctx.enter_context(nc.semaphore(name))

        pad_dram = nc.dram_tensor("filters_padded", [2, CH, PAD], F32, kind="Internal")

        par = sb("par", [P, NPARAM])
        freq_turns = sb("freq_turns", [P, 1])
        ones = sb("ones", [P, P], F32R)
        minus_half = sb("minus_half", [P, 1])

        xt_sb = sb("xt_sb", [P, XR, IMGS, BLOCKS, SIDE])
        x_sb = sb("x_sb", [P, 4, BLOCKS, PAIR, SIDE])
        xh = sb("xh", [P, 4, PAIR, BLOCKS, SIDE], F32R)
        xl = sb("xl", [P, 4, PAIR, BLOCKS, SIDE], F32R)
        toep_whole = sb("toep_whole", [P, XR, 2, SIDE])
        toep = sb("toep", [P, 2, 2, 2, SIDE], F32R)
        uh = sb("uh", [P, 2, BLOCKS, PAIR, SIDE], F32R)
        ul = sb("ul", [P, 2, BLOCKS, PAIR, SIDE], F32R)
        z_sb = sb("z_sb", [P, XR, 2, BLOCKS, PAIR, SIDE])
        out_sb = sb("out_sb", [P, 2, BLOCKS, PAIR, SIDE])
        zh = sb("zh", [P, 2, BLOCKS, PAIR, SIDE], F32R)
        zl = sb("zl", [P, 2, BLOCKS, PAIR, SIDE], F32R)
        w_sb = sb("w_sb", [P, 2, BLOCKS, SIDE])
        wh = sb("wh", [P, 2, BLOCKS, SIDE], F32R)
        wl = sb("wl", [P, 2, BLOCKS, SIDE], F32R)
        products = sb("products", [P, 2, BLOCKS, PAIR, SIDE], mybir.dt.bfloat16)
        red = sb("red", [P, XR, GROUPS])
        stat = sb("stat", [P, XR, GROUPS, 6])
        mv = sb("mv", [P, XR, 2])
        dev = sb("dev", [P, XR, 1])
        moment = sb("moment", [P, XR, 1])
        to_average = sb("to_average", [P, XR, 4], F32R)
        averages = sb("averages", [P, XR, 2])
        veps = sb("veps", [P, XR, 1])
        rstd = sb("rstd", [P, XR, 1])
        gain = sb("gain", [P, XR, 1])
        spacer = sb("spacer", [P, 1])
        centred = sb("centred", [P, XR, GROUPS])
        shift0 = sb("shift0", [P, XR, GROUPS])
        shift = sb("shift", [P, XR, GROUPS])

        early = [z_sb[:, i].rearrange("p c k b w -> p (c k b w)") for i in range(XR)]
        filt = early[2][:, 0:PAD]
        arg, turns, part, hid = (early[3][:, i * SIDE:(i + 1) * SIDE] for i in range(4))

        HALVES = [slice(P * i, P * (i + 1)) for i in range(2)]

        ps_u = ps("ps_u", [P, BLOCKS, PAIR, SIDE])
        ps_z = ps("ps_z", [P, BLOCKS, PAIR, SIDE])
        ps_c = ps("ps_c", [P, BLOCKS, PAIR, SIDE])
        ps_avg = ps("ps_avg", [P, 4])

        first_landed = sem("first_landed")
        weights_landed = sem("weights_landed")
        rest_landed = sem("rest_landed")
        const_ready = sem("const_ready")
        layer_done = sem("layer_done")
        reduced = sem("reduced")
        hid_ready = sem("hid_ready")
        filt_ready = sem("filt_ready")
        filt_stored = sem("filt_stored")
        xt_landed = [sem(f"xt_landed{i}") for i in range(XR)]
        x_landed = [sem(f"x_landed{i}") for i in range(4)]
        t_landed = [sem(f"t_landed{i}") for i in range(XR)]
        w_landed = [sem(f"w_landed{i}") for i in range(2)]
        th_ready = sem("th_ready")
        tl_ready = sem("tl_ready")
        xh_ready = sem("xh_ready")
        xl_ready = sem("xl_ready")
        wh_ready = sem("wh_ready")
        wl_ready = sem("wl_ready")
        u_done = sem("u_done")
        uh_ready = sem("uh_ready")
        ul_ready = sem("ul_ready")
        y_done = sem("y_done")
        z_ready = sem("z_ready")
        zh_ready = sem("zh_ready")
        zl_ready = sem("zl_ready")
        c_done = sem("c_done")
        bn_ready = sem("bn_ready")
        red_ready = sem("red_ready")
        shifted = sem("shifted")
        mv_ready = sem("mv_ready")
        mean_high = sem("mean_high")
        mean_in = sem("mean_in")
        averaged = sem("averaged")
        averages_ready = sem("averages_ready")
        dev_ready = sem("dev_ready")
        moment_ready = sem("moment_ready")
        moment_high = sem("moment_high")
        moment_in = sem("moment_in")
        veps_ready = sem("veps_ready")
        rstd_ready = sem("rstd_ready")
        gain_ready = sem("gain_ready")
        centred_ready = sem("centred_ready")
        shift0_ready = sem("shift0_ready")
        shift_ready = sem("shift_ready")
        norm_done = sem("norm_done")
        last_done = sem("last_done")
        stored = [sem(f"stored{h}") for h in range(2)]

        def chan_value(kind, st):
            return par[:, bass.ds(st.channel(COL_CHAN + kind * CH), 1)]

        def u_bank(us):
            return ps_c if second_pair(us) else ps_u

        block = ctx.enter_context(nc.Block())

        @block.sync
        def _(sp):
            for start, end, landed in ((0, COL_W2, first_landed), (COL_W2, COL_DECAY, weights_landed),
                                       (COL_DECAY, NPARAM, rest_landed)):
                sp.dma_start(par[:, start:end], params[:, start:end]).then_inc(landed, 16)

            def load_xt(m, slot):
                sp.dma_start(xt_sb[:, slot, :, :, :].rearrange("p b k h -> p (b k h)"),
                             xt[m, :, :, :, :].rearrange("p b k h -> p (b k h)"))\
                    .then_inc(xt_landed[slot], 16)

            def load_x(m, h, slot):
                sp.dma_start(x_sb[:, slot, :, :, :].rearrange("p k b w -> p (k b w)"),
                             x[m, :, h, :, :, :].rearrange("p k b w -> p (k b w)"))\
                    .then_inc(x_landed[slot], 16)

            def load_w(m, slot):
                sp.dma_start(w_sb[:, slot, :, :].rearrange("p k w -> p (k w)"),
                             wt[m, :, :, :].rearrange("p k w -> p (k w)"))\
                    .then_inc(w_landed[slot], 16)

            def load_toeplitz(m, slot):
                src = bass.AP(pad_dram, m * PAD + 1, [[1, P], [CH * PAD, 2], [1, SIDE]])
                sp.dma_start(toep_whole[:, slot, :, :], src).then_inc(t_landed[slot], 16)

            load_xt(0, 0)
            load_w(0, 0)
            load_xt(1, 1)
            sp.wait_ge(filt_ready, 1)
            sp.dma_start(pad_dram[:, :, :].rearrange("f c n -> (f c) n"), filt[:, :])\
                .then_inc(filt_stored, 16)
            sp.wait_ge(filt_stored, 16)

            def stage(st):
                done = st.trail(LAG_STORE)
                if active(done):
                    m, h = done.channel(), done.half()
                    normed = z_sb[:, done.ring(XR), h] if ending(done, 4) else out_sb[:, h]
                    if ending(done, 3):
                        sp.wait_ge(last_done, done.number() - (PAIRS - 3) + 1)
                    else:
                        wait(sp, norm_done, done, 1)
                    sp.dma_start(out[m, :, h, :, :, :].rearrange("p k b w -> p (k b w)"),
                                 normed.rearrange("p k b w -> p (k b w)"))\
                        .then_inc(stored[h], 16)
                ts = st.trail(LAG_LOAD_T)
                if starts(ts):
                    wait(sp, u_done, ts, -2 * XR + 2)
                    load_toeplitz(ts.channel(), ts.ring(XR))
                ws = st.trail(LAG_LOAD_W)
                if starts(ws) and not (ws.static() and ws.channel() < 1):
                    wait_chan(sp, wl_ready, ws, -1)
                    load_w(ws.channel(), ws.ring(2))
                xs = st.trail(LAG_LOAD_X)
                if active(xs):
                    wait(sp, z_ready, xs, -3)
                    load_x(xs.channel(), xs.half(), xs.slot(4))
                ts = st.trail(LAG_LOAD_XT)
                if starts(ts) and not (ts.static() and ts.channel() < 2):
                    wait(sp, u_done, ts, -2 * XR + 2)
                    load_xt(ts.channel(), ts.ring(XR))

            run_steps(sp, PAIRS, 2 * UNROLL, LAG_STORE, stage)
            for h in range(2):
                sp.wait_ge(stored[h], 16 * CH)

        @block.gpsimd
        def _(pool):
            nc.gpsimd.memset(filt[:, 0:P], 0.0).then_inc(const_ready, 1)
            nc.gpsimd.memset(ones[:, :].bitcast(F32), 1.0 / P).then_inc(const_ready, 1)
            nc.gpsimd.memset(minus_half[:, :], -0.5).then_inc(const_ready, 1)
            nc.gpsimd.memset(to_average[:, :, :].bitcast(F32), 0.0).then_inc(const_ready, 1)
            pool.wait_ge(const_ready, 4)

            def stage(st):
                co = st.trail(LAG_NORM)
                if starts(co):
                    r = co.ring(XR)
                    wait_chan(pool, veps_ready, co, 2)
                    nc.gpsimd.tensor_tensor(rstd[:, r], veps[:, r], minus_half[:, :], ALU.pow)\
                        .then_inc(rstd_ready, 1)
                    wait_chan(pool, rstd_ready, co, 1)
                    nc.gpsimd.tensor_tensor(gain[:, r], rstd[:, r], chan_value(1, co), ALU.mult)\
                        .then_inc(gain_ready, 1)
                    wait_chan(pool, averages_ready, co, 1 + ending(co, 4) + ending(co, 2))
                    nc.gpsimd.tensor_tensor(centred[:, r], red[:, r],
                                            averages[:, r, 0:1].broadcast_to([P, GROUPS]), ALU.subtract)\
                        .then_inc(centred_ready, 1)
                    wait_chan(pool, gain_ready, co, 1)
                    wait_chan(pool, centred_ready, co, 1)
                    nc.gpsimd.tensor_tensor(shift0[:, r], centred[:, r],
                                            gain[:, r].broadcast_to([P, GROUPS]), ALU.mult)\
                        .then_inc(shift0_ready, 1)
                    wait_chan(pool, shift0_ready, co, 1)
                    nc.gpsimd.tensor_tensor(shift[:, r], shift0[:, r],
                                            chan_value(2, co).broadcast_to([P, GROUPS]), ALU.add)\
                        .then_inc(shift_ready, 1)

                if active(st):
                    wait(pool, xh_ready, st, 1)
                    r, h = st.ring(XR), st.half()
                    nc.gpsimd.tensor_tensor(xl[:, st.slot(4)], xt_sb[:, r, PAIR * h:PAIR * (h + 1)],
                                            xh[:, st.slot(4)].bitcast(F32), ALU.subtract)\
                        .then_inc(xl_ready, 1)
                ws = st.trail(LAG_W)
                if starts(ws):
                    r = ws.ring(2)
                    wait_chan(pool, wh_ready, ws, 1)
                    nc.gpsimd.tensor_tensor(wl[:, r], w_sb[:, r], wh[:, r].bitcast(F32),
                                            ALU.subtract).then_inc(wl_ready, 1)
                zs = st.trail(LAG_Z)
                if active(zs) and not ending(zs, 2):
                    wait(pool, zh_ready, zs, 1)
                    r, h = zs.ring(XR), zs.half()
                    nc.gpsimd.tensor_tensor(zl[:, zs.slot(2)], z_sb[:, r, h],
                                            zh[:, zs.slot(2)].bitcast(F32), ALU.subtract)\
                        .then_inc(zl_ready, 1)
            run_steps(pool, PAIRS, 2 * UNROLL, LAG_NORM + 1, stage)

        @block.scalar
        def _(act):
            for layer in range(3):
                for i, half in enumerate(HALVES):
                    act.wait_ge(reduced, 6 * layer + 6 + i)
                    nc.scalar.activation(hid[:, half], part[:, half], ACT.Sin, scale=TWO_PI_BELOW)\
                        .then_inc(hid_ready, 1)

            def stage(st):
                if active(st):
                    r, h = st.ring(XR), st.half()
                    if h == 0:
                        act.wait_ge(xt_landed[r], st.turn(XR) * 16)
                    wait(act, u_done, st, -3)
                    nc.scalar.activation(xh[:, st.slot(4)], xt_sb[:, r, PAIR * h:PAIR * (h + 1)],
                                         ACT.Copy).then_inc(xh_ready, 1)
                ts = st.trail(LAG_T)
                if starts(ts):
                    r = ts.ring(XR)
                    act.wait_ge(t_landed[r], ts.turn(XR) * 16)
                    wait(act, y_done, ts, -2)
                    nc.scalar.activation(toep[:, ts.ring(2), :, 0], toep_whole[:, r], ACT.Copy)\
                        .then_inc(th_ready, 1)
                ws = st.trail(LAG_W)
                if starts(ws):
                    r = ws.ring(2)
                    act.wait_ge(w_landed[r], ws.turn(2) * 16)
                    wait(act, c_done, ws, -2)
                    nc.scalar.activation(wh[:, r], w_sb[:, r], ACT.Copy).then_inc(wh_ready, 1)
                us = st.trail(LAG_U)
                if active(us):
                    wait(act, u_done, us, 1)
                    wait(act, y_done, us, -1)
                    nc.scalar.activation(uh[:, us.slot(2)], u_bank(us)[:, :, :, :], ACT.Copy)\
                        .then_inc(uh_ready, 1)
                no = st.trail(LAG_NORM)
                if active(no) and not ending(no, 3):
                    if no.first_of_channel():
                        wait_chan(act, shift_ready, no, 1)
                    r, h = no.ring(XR), no.half()
                    to = out_sb[:, h]
                    if ending(no, 4):
                        to = z_sb[:, r, h]
                    elif not no.static() or no.channel() > 0:
                        act.wait_ge(stored[h], no.channel() * 16)
                    for k in range(BLOCKS):
                        for b in range(PAIR):
                            g = (h * BLOCKS + k) * PAIR + b
                            last = nc.scalar.activation(to[:, k, b], z_sb[:, r, h, k, b], ACT.Identity,
                                                        bias=shift[:, r, g:g + 1], scale=gain[:, r])
                    last.then_inc(norm_done, 1)
                zs = st.trail(LAG_Z)
                if active(zs):
                    wait(act, z_ready, zs, 1)
                    wait(act, c_done, zs, -1)
                    r, h = zs.ring(XR), zs.half()
                    nc.scalar.activation(zh[:, zs.slot(2)], z_sb[:, r, h],
                                         ACT.Copy).then_inc(zh_ready, 1)

            run_steps(act, PAIRS, 2 * UNROLL, LAG_NORM, stage)

        @block.tensor
        def _(pe):
            def mm(o, a, b, start, stop):
                return nc.tensor.matmul(o, a, b, start=start, stop=stop)

            def keep_warm(count):
                for _ in range(count):
                    mm(ps_c[:, 0], ones[:, :],
                       ones[:, :].unsqueeze(1).broadcast_to([P, SIDE * PAIR // P, P]), True, True)

            pe.wait_ge(const_ready, 4)
            keep_warm(WARM_FIRST)
            pe.wait_ge(first_landed, 16)
            for i, half in enumerate(HALVES):
                mm(ps_u[:, i, 0, 0:P], par[0:EMB, COL_W1:COL_W1 + P],
                   par[0:EMB, COL_ZT + half.start:COL_ZT + half.stop], True, True).then_inc(layer_done, 1)
            pe.wait_ge(weights_landed, 16)
            for layer, col in enumerate((COL_W2, COL_W3, COL_WO)):
                keep_warm(WARM_LAYER)
                for i, half in enumerate(HALVES):
                    pe.wait_ge(hid_ready, 2 * layer + 1 + i)
                    mm(ps_u[:, i, 0, 0:P], par[:, col:col + P], hid[:, half], True, True)\
                        .then_inc(layer_done, 1)
            pe.wait_ge(filt_ready, 1)
            keep_warm(WARM_TOEPLITZ)

            def product_y(zs):
                wait(pe, ul_ready, zs, 1)
                wait(pe, z_ready, zs, 0)
                s, t = zs.slot(2), zs.ring(2)
                for a in range(BLOCKS):
                    for h in range(a + 1):
                        cols = slice(P * (a - h), P * (a - h + 1))
                        t_h, t_l = toep[:, t, 0, 0, cols], toep[:, t, 0, 1, cols]
                        mm(ps_z[:, a], t_h, uh[:, s, h], h == 0, False)
                        mm(ps_z[:, a], t_h, ul[:, s, h], False, False)
                        last = mm(ps_z[:, a], t_l, uh[:, s, h], False, h == a)
                last.then_inc(y_done, 1)

            def product_c(cs, bank):
                wait_chan(pe, wl_ready, cs, 1)
                wait(pe, zl_ready, cs, 1)
                s, w = cs.slot(2), cs.ring(2)
                for a in range(BLOCKS):
                    for k in range(BLOCKS):
                        w_h, w_l = wh[:, w, k, P * a:P * (a + 1)], wl[:, w, k, P * a:P * (a + 1)]
                        mm(bank[:, a], w_h, zh[:, s, k], k == 0, False)
                        mm(bank[:, a], w_h, zl[:, s, k], False, False)
                        last = mm(bank[:, a], w_l, zh[:, s, k], False, k == BLOCKS - 1)
                last.then_inc(c_done, 1)

            def average(slot):
                mm(ps_avg[:, :], ones[:, :], to_average[:, slot], True, True).then_inc(averaged, 1)

            def stage(st):
                us = st.trail(LAG_U)
                if active(us):
                    r, t = us.ring(XR), us.ring(2)
                    if us.first_of_channel():
                        wait_chan(pe, tl_ready, us, 1)
                    wait(pe, xl_ready, us, 1)
                    if not second_pair(us):
                        wait(pe, ul_ready, us, 0)
                    s = us.slot(4)
                    for h in range(BLOCKS):
                        rows = slice(P * h, P * (h + 1))
                        for b in range(PAIR):
                            o = u_bank(us)[:, h, b, :]
                            mm(o, xh[:, s, b, 0, rows], toep[:, t, 1, 0, :], True, False)
                            mm(o, xh[:, s, b, 0, rows], toep[:, t, 1, 1, :], False, False)
                            mm(o, xl[:, s, b, 0, rows], toep[:, t, 1, 0, :], False, False)
                            last = mm(o[:, P:SIDE], xt_sb[:, r, PAIR * us.half() + b, 1, rows],
                                      toep_whole[:, r, 1, 0:P], False, True)
                    last.then_inc(u_done, 1)
                zs = st.trail(LAG_Z)
                if active(zs):
                    product_y(zs)
                cs = st.trail(LAG_RED)
                if active(cs):
                    wait(pe, red_ready, cs, 0)
                    product_c(cs, ps_c)
                ms = st.trail(LAG_MEAN)
                if starts(ms):
                    wait_chan(pe, mean_in, ms, 1)
                    wait_chan(pe, moment_in, ms, 0)
                    wait_chan(pe, averages_ready, ms, 0)
                    average(ms.ring(XR))

            run_steps(pe, PAIRS, UNROLL, END_STEPS, stage)
            end = [Step(0, i) for i in range(PAIRS - 2, PAIRS)]
            product_y(end[1])
            pe.wait_ge(moment_in, CH - 2)
            pe.wait_ge(averages_ready, CH - 2)
            average((CH - 2) % XR)
            pe.wait_ge(red_ready, PAIRS - 2)
            product_c(end[0], ps_c)
            product_c(end[1], ps_u)
            for i, channel in enumerate((CH - 2, CH - 1)):
                pe.wait_ge(mean_in, channel + 1)
                pe.wait_ge(averages_ready, CH - 1 + 2 * i)
                average(channel % XR)
                pe.wait_ge(moment_in, channel + 1)
                pe.wait_ge(averages_ready, CH + 2 * i)
                average((channel + 1) % XR)

        @block.vector
        def _(dve):
            dve.wait_ge(first_landed, 16)
            nc.vector.tensor_scalar(freq_turns[:, :], par[:, COL_FREQ:COL_FREQ + 1], 1.0 / (2.0 * math.pi),
                                    None, ALU.mult).then_inc(reduced, 1)
            for layer in range(3):
                for i, half in enumerate(HALVES):
                    dve.wait_ge(layer_done, 2 * layer + 1 + i)
                    dve.wait_ge(reduced, 6 * layer + 1 + i)
                    nc.vector.tensor_scalar(arg[:, half], ps_u[:, i, 0, 0:P],
                                            par[:, COL_BIAS + layer:COL_BIAS + layer + 1],
                                            freq_turns[:, 0:1], ALU.add, ALU.mult).then_inc(reduced, 1)
                for i, half in enumerate(HALVES):
                    dve.wait_ge(reduced, 6 * layer + 2 + i)
                    nc.vector.tensor_scalar(turns[:, half], arg[:, half], ROUND_MAGIC, ROUND_MAGIC,
                                            ALU.add, ALU.subtract).then_inc(reduced, 1)
                for i, half in enumerate(HALVES):
                    dve.wait_ge(reduced, 6 * layer + 4 + i)
                    if layer > 0:
                        dve.wait_ge(hid_ready, 2 * layer - 1 + i)
                    nc.vector.tensor_tensor(part[:, half], arg[:, half], turns[:, half], ALU.subtract)\
                        .then_inc(reduced, 1)
            dve.wait_ge(layer_done, 8)
            dve.wait_ge(rest_landed, 16)
            dve.wait_ge(const_ready, 4)
            nc.vector.tensor_tensor(filt[:, P:PAD].rearrange("p (i n) -> p i n", i=2), ps_u[:, :, 0, 0:P],
                                    par[:, COL_DECAY:COL_DECAY + SIDE].rearrange("p (i n) -> p i n", i=2),
                                    ALU.mult).then_inc(filt_ready, 1)

            def read_averages(slot):
                nc.vector.tensor_reduce(averages[:, slot].unsqueeze(2),
                                        ps_avg[:, :].rearrange("p (q h) -> p q h", h=2),
                                        mybir.AxisListType.X, ALU.add).then_inc(averages_ready, 1)

            def add_epsilon(slot):
                nc.vector.tensor_scalar(veps[:, (slot - 1) % XR], averages[:, slot, 1:2], BN_EPS, None,
                                        ALU.add).then_inc(veps_ready, 1)

            def second_moment(vs):
                r, after = vs.ring(XR), (vs.ring(XR) + 1) % XR
                nc.vector.tensor_scalar(dev[:, r], mv[:, r, 0:1], averages[:, r, 0:1], None,
                                        ALU.subtract).then_inc(dev_ready, 1)
                wait_chan(dve, dev_ready, vs, 1)
                nc.vector.scalar_tensor_tensor(out=moment[:, r], in0=dev[:, r], scalar=dev[:, r],
                                               in1=mv[:, r, 1:2], op0=ALU.mult, op1=ALU.add)\
                    .then_inc(moment_ready, 1)
                wait_chan(dve, moment_ready, vs, 1)
                nc.vector.tensor_copy(to_average[:, after, 2:3], moment[:, r]).then_inc(moment_high, 1)
                wait_chan(dve, moment_high, vs, 1)
                nc.vector.tensor_tensor(to_average[:, after, 3:4], moment[:, r],
                                        to_average[:, after, 2:3].bitcast(F32), ALU.subtract)\
                    .then_inc(moment_in, 1)

            def mean_of_partition(ms):
                r = ms.ring(XR)
                wait(dve, red_ready, ms, 2)
                wait(dve, bn_ready, ms, 2)
                means = stat[:, r].rearrange("p g (h s) -> p g h s", h=2)[:, :, :, 1]
                nc.vector.tensor_tensor(
                    means, means,
                    red[:, r].unsqueeze(2).broadcast_to([P, GROUPS, 2]),
                    ALU.add).then_inc(shifted, 1)
                wait_chan(dve, shifted, ms, 1)
                nc.vector.memset(spacer[:, :], 0.0)
                nc.vector.bn_aggr(mv[:, r], stat[:, r].rearrange("p g s -> p (g s)"))\
                    .then_inc(mv_ready, 1)
                wait_chan(dve, mv_ready, ms, 1)
                nc.vector.tensor_copy(to_average[:, r, 0:1], mv[:, r, 0:1]).then_inc(mean_high, 1)
                wait_chan(dve, mean_high, ms, 1)
                nc.vector.tensor_tensor(to_average[:, r, 1:2], mv[:, r, 0:1],
                                        to_average[:, r, 0:1].bitcast(F32), ALU.subtract)\
                    .then_inc(mean_in, 1)

            def whole_z(zs):
                r, h = zs.ring(XR), zs.half()
                dve.wait_ge(x_landed[zs.slot(4)], zs.turn(2) * 16)
                wait(dve, norm_done, zs, 1 - 2 * XR)
                wait(dve, y_done, zs, 1)
                nc.vector.scalar_tensor_tensor(
                    out=z_sb[:, r, h].rearrange("p k b w -> p (k b w)"),
                    in0=x_sb[:, zs.slot(4)].rearrange("p k b w -> p (k b w)"),
                    scalar=chan_value(0, zs), in1=ps_z[:, :, :, :].rearrange("p k b w -> p (k b w)"),
                    op0=ALU.mult, op1=ALU.add).then_inc(z_ready, 1)

            def low_z(zs):
                wait(dve, zh_ready, zs, 1)
                wait(dve, zl_ready, zs, 0)
                nc.vector.tensor_tensor(zl[:, zs.slot(2)], z_sb[:, zs.ring(XR), zs.half()],
                                        zh[:, zs.slot(2)].bitcast(F32), ALU.subtract)\
                    .then_inc(zl_ready, 1)

            def reduce_rows(cs, bank):
                r, h = cs.ring(XR), cs.half()
                wait(dve, c_done, cs, 1)
                for k in range(BLOCKS):
                    for b in range(PAIR):
                        g = (h * BLOCKS + k) * PAIR + b
                        last = nc.vector.tensor_tensor_reduce(
                            products[:, cs.slot(2), k, b], z_sb[:, r, h, k, b], bank[:, k, b],
                            1.0 / math.sqrt(SIDE), 0.0, ALU.mult, ALU.add, red[:, r, g:g + 1])
                last.then_inc(red_ready, 1)

            def statistics(zs):
                wait(dve, z_ready, zs, 1)
                r, h = zs.ring(XR), zs.half()
                for k in range(BLOCKS):
                    for b in range(PAIR):
                        last = nc.vector.bn_stats(stat[:, r, (h * BLOCKS + k) * PAIR + b],
                                                  z_sb[:, r, h, k, b])
                last.then_inc(bn_ready, 1)

            def stage(st):
                vs = st.trail(LAG_SPREAD)
                if starts(vs):
                    wait_chan(dve, averaged, vs, 1)
                    read_averages(vs.ring(XR))
                    wait_chan(dve, averages_ready, vs, 1)
                    add_epsilon(vs.ring(XR))
                    second_moment(vs)
                ts = st.trail(LAG_T)
                if starts(ts):
                    t = ts.ring(2)
                    wait_chan(dve, th_ready, ts, 1)
                    nc.vector.tensor_tensor(toep[:, t, :, 1], toep_whole[:, ts.ring(XR)],
                                            toep[:, t, :, 0].bitcast(F32), ALU.subtract)\
                        .then_inc(tl_ready, 1)
                ms = st.trail(LAG_MEAN)
                if starts(ms):
                    mean_of_partition(ms)
                us = st.trail(LAG_U)
                if active(us):
                    wait(dve, uh_ready, us, 1)
                    nc.vector.tensor_tensor(ul[:, us.slot(2)], u_bank(us)[:, :, :, :],
                                            uh[:, us.slot(2)].bitcast(F32), ALU.subtract)\
                        .then_inc(ul_ready, 1)
                zs = st.trail(LAG_Z)
                if active(zs):
                    whole_z(zs)
                cs = st.trail(LAG_RED)
                if active(cs):
                    reduce_rows(cs, ps_c)
                if active(zs) and not ending(zs, 2):
                    statistics(zs)

            run_steps(dve, PAIRS, 2 * UNROLL, END_STEPS, stage)
            end = [Step(0, i) for i in range(PAIRS - 2, PAIRS)]
            before, final = Step(0, PAIRS - 4), Step(0, PAIRS - 2)

            def next_average(count, slot):
                dve.wait_ge(averaged, count)
                read_averages(slot)
                dve.wait_ge(averages_ready, count)

            low_z(end[0])
            whole_z(end[1])
            next_average(CH - 1, before.ring(XR))
            add_epsilon(before.ring(XR))
            statistics(end[0])
            low_z(end[1])
            reduce_rows(end[0], ps_c)
            mean_of_partition(before)
            statistics(end[1])
            next_average(CH, before.ring(XR))
            second_moment(before)
            reduce_rows(end[1], ps_u)
            next_average(CH + 1, final.ring(XR))
            add_epsilon(final.ring(XR))
            mean_of_partition(final)
            next_average(CH + 2, final.ring(XR))
            second_moment(final)
            next_average(CH + 3, CH % XR)
            add_epsilon(CH % XR)
            for i in range(PAIRS - 3, PAIRS):
                r, h = i // 2 % XR, i % 2
                dve.wait_ge(shift_ready, i // 2 + 1)
                for k in range(BLOCKS):
                    for b in range(PAIR):
                        g = (h * BLOCKS + k) * PAIR + b
                        rows = z_sb[:, r, h, k, b]
                        last = nc.vector.tensor_scalar(rows, rows, gain[:, r], shift[:, r, g:g + 1],
                                                       ALU.mult, ALU.add)
                last.then_inc(last_done, 1)


def decay_rows(channels):
    t = np.linspace(0.0, 1.0, SIDE).astype(np.float32)
    deltas = np.linspace(math.log(0.01) / 1.5, math.log(0.01) / 0.3, channels).astype(np.float32)
    decay = np.exp((-t[None, :] * np.abs(deltas)[:, None]).astype(np.float32))
    return np.concatenate([decay, decay / np.float32(2 * SIDE)]).astype(np.float32)


def kernel(**inputs):
    import concourse.bacc as bacc
    from concourse.bass_utils import run_bass_kernel_spmd

    a = {k: np.asarray(v) for k, v in inputs.items()}
    x = a["x"]
    imgs, ch = x.shape[:2]

    x_in = np.ascontiguousarray(
        x.reshape(2, imgs // 2, ch, BLOCKS, P, SIDE).transpose(2, 4, 0, 3, 1, 5))
    xt_in = np.ascontiguousarray(
        x.reshape(imgs, ch, BLOCKS, P, BLOCKS, P)[:, :, :, ::-1, :, ::-1].transpose(1, 5, 0, 4, 2, 3)
    ).reshape(ch, P, imgs, BLOCKS, SIDE)
    wt_in = np.ascontiguousarray(
        a["L1_conv_weights"].reshape(ch, SIDE, BLOCKS, P).transpose(0, 3, 2, 1))
    params = np.zeros((P, COL_CHAN + 3 * ch), np.float32)
    params[0:EMB, COL_ZT:COL_ZT + SIDE] = a["L0_conv_z"][0].T
    params[0:EMB, COL_W1:COL_W1 + ORDER] = a["L0_conv_Xw1"]
    params[0:EMB, COL_W1 + ORDER:COL_W1 + P] = a["L0_conv_Yw1"]
    for col, name in ((COL_W2, "w2"), (COL_W3, "w3"), (COL_WO, "wo")):
        params[0:ORDER, col:col + ORDER] = a["L0_conv_X" + name]
        params[ORDER:P, col + ORDER:col + P] = a["L0_conv_Y" + name]
    for i, name in enumerate(("b1", "b2", "b3", "freq")):
        params[0:ORDER, COL_BIAS + i] = a["L0_conv_X" + name].reshape(-1)
        params[ORDER:P, COL_BIAS + i] = a["L0_conv_Y" + name].reshape(-1)
    params[:, COL_DECAY:COL_DECAY + SIDE] = decay_rows(ch)
    for i, name in enumerate(("L0_conv_bias", "L1_conv_gamma", "L1_conv_beta")):
        params[:, COL_CHAN + i * ch:COL_CHAN + (i + 1) * ch] = a[name][None, :]

    arrays = {"x_in": x_in, "xt_in": xt_in, "wt_in": wt_in, "params_in": params}
    nc = bacc.Bacc("TRN2", target_bir_lowering=False, num_devices=1)
    args = [nc.dram_tensor(n, v.shape, mybir.dt.from_np(v.dtype), kind="ExternalInput").ap()
            for n, v in arrays.items()]
    out = nc.dram_tensor("out", x_in.shape, F32, kind="ExternalOutput").ap()
    build(nc, *args, out)
    r = run_bass_kernel_spmd(nc, [arrays], core_ids=[0])
    y = r.results[0]["out"]
    return np.ascontiguousarray(y.transpose(2, 4, 0, 3, 1, 5)).reshape(x.shape)
```
